# Optimizing a Trainium2 kernel written in Bass

```python
import numpy as np
import jax
import jax.numpy as jnp

def _softmax(x, axis=-1):
    return jax.nn.softmax(x, axis=axis)

def _gelu(x):
    return jax.nn.gelu(x, approximate=True)

def _silu(x):
    return jax.nn.silu(x)

def _sigmoid(x):
    return jax.nn.sigmoid(x)

def _layernorm(x, axis=-1, eps=1e-05):
    m = jnp.mean(x, axis=axis, keepdims=True)
    v = jnp.var(x, axis=axis, keepdims=True)
    return (x - m) / jnp.sqrt(v + eps)

def _scatter_add(tgt, idx, src, axis=0):
    return tgt.at[idx].add(src)

def _segment_sum(src, seg, n):
    return jax.ops.segment_sum(src, seg, n)
kernel_name = 'mk_adj_ffn_d2_adj_r2_2debf4'

def setup_inputs(seed: int=0):
    np.random.seed(seed)
    _w = jnp.asarray

    def _rec_inputs():
        import jax
        import jax.numpy as jnp
        _gk = jax.random.key(seed)
        x = -0.0003929 + 0.9999 * jax.random.normal(jax.random.fold_in(_gk, 1), (16, 512, 128), jnp.float32)
        _w = (1.0 + jnp.arange(512, dtype=jnp.float32)) ** (-0.5)
        _w = _w / _w.mean()
        _pij = jnp.clip(0.00390625 * _w[:, None] * _w[None, :], 0.0, 1.0)
        _a = jax.random.uniform(jax.random.fold_in(_gk, 2), (512, 512)) < _pij
        _a = jnp.logical_or(_a, jnp.swapaxes(_a, -1, -2))
        _a = jnp.logical_or(_a, jnp.eye(512, dtype=bool))
        _af = _a.astype(jnp.float32)
        _af = _af * jax.random.uniform(jax.random.fold_in(_gk, 3), (512, 512), jnp.float32, 0.05, 1)
        adj = _af
        return (x, adj)
    x, adj = _rec_inputs()

    def _L0_gnn_setup():
        import jax, jax.numpy as jnp
        import numpy as np
        EPS = 1e-05

        def _batchnorm(x, gamma, beta):
            mu = jnp.mean(x, axis=0)
            var = jnp.var(x, axis=0)
            return (x - mu) * jax.lax.rsqrt(var + EPS) * gamma + beta
        key = jax.random.key(seed)
        ks = jax.random.split(key, 4)
        b, n, d, h, o = (32, 1024, 128, 256, 128)
        features = jax.random.normal(ks[0], (b, n, d), dtype=jnp.float32)
        A = jax.random.uniform(ks[1], (n, n), dtype=jnp.float32)
        lim1 = float(np.sqrt(6.0 / (d + h)))
        W1 = jax.random.uniform(ks[2], (h, d), minval=-lim1, maxval=lim1, dtype=jnp.float32)
        b1 = jnp.zeros((h,), jnp.float32)
        lim2 = float(np.sqrt(6.0 / (h + o)))
        W2 = jax.random.uniform(ks[3], (o, h), minval=-lim2, maxval=lim2, dtype=jnp.float32)
        b2 = jnp.zeros((o,), jnp.float32)
        g1 = jnp.ones((h,), jnp.float32)
        be1 = jnp.zeros((h,), jnp.float32)
        g2 = jnp.ones((o,), jnp.float32)
        be2 = jnp.zeros((o,), jnp.float32)
        return {'features': features, 'A': A, 'W1': W1, 'b1': b1, 'g1': g1, 'be1': be1, 'W2': W2, 'b2': b2, 'g2': g2, 'be2': be2}
    _L0_gnn_all = _L0_gnn_setup()
    _L0_gnn_in = {k: v for k, v in _L0_gnn_all.items() if k in ('W1', 'b1', 'g1', 'be1', 'W2', 'b2', 'g2', 'be2')}
    del _L0_gnn_all

    def _L0_ffn_setup():
        import jax, jax.numpy as jnp
        import numpy as np
        B, S, D, H, E, K = (8, 4096, 128, 512, 8, 2)
        key = jax.random.key(seed)
        ks = jax.random.split(key, 7)
        s_in = 1.0 / np.sqrt(D)
        s_hid = 1.0 / np.sqrt(H)
        return {'x': jax.random.normal(ks[0], (B, S, D), dtype=jnp.float32), 'Wg': jax.random.uniform(ks[1], (E, D), jnp.float32, -s_in, s_in), 'bg': jax.random.uniform(ks[2], (E,), jnp.float32, -s_in, s_in), 'W1': jax.random.uniform(ks[3], (E, H, D), jnp.float32, -s_in, s_in), 'b1': jax.random.uniform(ks[4], (E, H), jnp.float32, -s_in, s_in), 'W2': jax.random.uniform(ks[5], (E, D, H), jnp.float32, -s_hid, s_hid), 'b2': jax.random.uniform(ks[6], (E, D), jnp.float32, -s_hid, s_hid)}
    _L0_ffn_all = _L0_ffn_setup()
    _L0_ffn_in = {k: v for k, v in _L0_ffn_all.items() if k in ('Wg', 'bg', 'W1', 'b1', 'W2', 'b2')}
    del _L0_ffn_all

    def _L1_gnn_setup():
        import jax, jax.numpy as jnp
        import numpy as np
        B, T, D, H = (64, 1024, 128, 128)
        MAX_SKIP = 4

        def _lstm_last(Wih, Whh, bih, bhh, xs):
            N, _, Hd = xs.shape
            bias = bih + bhh

            def step(carry, x_t):
                h, c = carry
                g = x_t @ Wih.T + h @ Whh.T + bias
                i, f, gg, o = jnp.split(g, 4, axis=-1)
                c = jax.nn.sigmoid(f) * c + jax.nn.sigmoid(i) * jnp.tanh(gg)
                h = jax.nn.sigmoid(o) * jnp.tanh(c)
                return ((h, c), None)
            init = (jnp.zeros((N, Hd), xs.dtype), jnp.zeros((N, Hd), xs.dtype))
            (h_last, _), _ = jax.lax.scan(step, init, jnp.swapaxes(xs, 0, 1))
            return h_last
        key = jax.random.key(seed)
        ks = jax.random.split(key, 8)
        s = 0.05
        x = jax.random.normal(ks[0], (B, T, D), jnp.float32)
        adj = jax.random.uniform(ks[1], (T, T), jnp.float32) / T
        Wg0 = jax.random.normal(ks[2], (D, H), jnp.float32) * s
        bg0 = jnp.zeros((H,), jnp.float32)
        Wg1 = jax.random.normal(ks[3], (H, H), jnp.float32) * s
        bg1 = jnp.zeros((H,), jnp.float32)
        Wih = jax.random.normal(ks[4], (MAX_SKIP, 4 * H, H), jnp.float32) * s
        Whh = jax.random.normal(ks[5], (MAX_SKIP, 4 * H, H), jnp.float32) * s
        bih = jax.random.normal(ks[6], (MAX_SKIP, 4 * H), jnp.float32) * s
        bhh = jax.random.normal(ks[7], (MAX_SKIP, 4 * H), jnp.float32) * s
        return dict(x=x, adj=adj, Wg0=Wg0, bg0=bg0, Wg1=Wg1, bg1=bg1, Wih=Wih, Whh=Whh, bih=bih, bhh=bhh)
    _L1_gnn_all = _L1_gnn_setup()
    _L1_gnn_in = {k: v for k, v in _L1_gnn_all.items() if k in ('Wg0', 'bg0', 'Wg1', 'bg1', 'Wih', 'Whh', 'bih', 'bhh')}
    del _L1_gnn_all

    def _L1_ffn_setup():
        import math
        import jax, jax.numpy as jnp
        import numpy as np
        CAPACITY_FACTOR = 1.25
        TOP_K = 2
        LN_EPS = 1e-05

        def _layer_norm(x, gamma, beta):
            mu = jnp.mean(x, axis=-1, keepdims=True)
            var = jnp.var(x, axis=-1, keepdims=True)
            return (x - mu) * jax.lax.rsqrt(var + LN_EPS) * gamma + beta
        key = jax.random.key(seed)
        ks = jax.random.split(key, 4)
        B, S, D, F, E = (8, 2048, 128, 256, 8)
        x = jax.random.normal(ks[0], (B, S, D), dtype=jnp.float32)
        Wr = jax.random.normal(ks[1], (D, E), dtype=jnp.float32) / np.sqrt(D)
        br = jnp.zeros((E,), jnp.float32)
        W1 = jax.random.normal(ks[2], (E, D, F), dtype=jnp.float32) / np.sqrt(D)
        b1 = jnp.zeros((E, F), jnp.float32)
        W2 = jax.random.normal(ks[3], (E, F, D), dtype=jnp.float32) / np.sqrt(F)
        b2 = jnp.zeros((E, D), jnp.float32)
        gamma = jnp.ones((D,), jnp.float32)
        beta = jnp.zeros((D,), jnp.float32)
        return {'x': x, 'Wr': Wr, 'br': br, 'W1': W1, 'b1': b1, 'W2': W2, 'b2': b2, 'gamma': gamma, 'beta': beta}
    _L1_ffn_all = _L1_ffn_setup()
    _L1_ffn_in = {k: v for k, v in _L1_ffn_all.items() if k in ('Wr', 'br', 'W1', 'b1', 'W2', 'b2', 'gamma', 'beta')}
    del _L1_ffn_all
    return {'x': x, 'adj': adj, 'L0_gnn_W1': _L0_gnn_in['W1'], 'L0_gnn_b1': _L0_gnn_in['b1'], 'L0_gnn_g1': _L0_gnn_in['g1'], 'L0_gnn_be1': _L0_gnn_in['be1'], 'L0_gnn_W2': _L0_gnn_in['W2'], 'L0_gnn_b2': _L0_gnn_in['b2'], 'L0_gnn_g2': _L0_gnn_in['g2'], 'L0_gnn_be2': _L0_gnn_in['be2'], 'L0_ffn_Wg': _L0_ffn_in['Wg'], 'L0_ffn_bg': _L0_ffn_in['bg'], 'L0_ffn_W1': _L0_ffn_in['W1'], 'L0_ffn_b1': _L0_ffn_in['b1'], 'L0_ffn_W2': _L0_ffn_in['W2'], 'L0_ffn_b2': _L0_ffn_in['b2'], 'L1_gnn_Wg0': _L1_gnn_in['Wg0'], 'L1_gnn_bg0': _L1_gnn_in['bg0'], 'L1_gnn_Wg1': _L1_gnn_in['Wg1'], 'L1_gnn_bg1': _L1_gnn_in['bg1'], 'L1_gnn_Wih': _L1_gnn_in['Wih'], 'L1_gnn_Whh': _L1_gnn_in['Whh'], 'L1_gnn_bih': _L1_gnn_in['bih'], 'L1_gnn_bhh': _L1_gnn_in['bhh'], 'L1_ffn_Wr': _L1_ffn_in['Wr'], 'L1_ffn_br': _L1_ffn_in['br'], 'L1_ffn_W1': _L1_ffn_in['W1'], 'L1_ffn_b1': _L1_ffn_in['b1'], 'L1_ffn_W2': _L1_ffn_in['W2'], 'L1_ffn_b2': _L1_ffn_in['b2'], 'L1_ffn_gamma': _L1_ffn_in['gamma'], 'L1_ffn_beta': _L1_ffn_in['beta']}

def reference(x, adj, L0_gnn_W1, L0_gnn_b1, L0_gnn_g1, L0_gnn_be1, L0_gnn_W2, L0_gnn_b2, L0_gnn_g2, L0_gnn_be2, L0_ffn_Wg, L0_ffn_bg, L0_ffn_W1, L0_ffn_b1, L0_ffn_W2, L0_ffn_b2, L1_gnn_Wg0, L1_gnn_bg0, L1_gnn_Wg1, L1_gnn_bg1, L1_gnn_Wih, L1_gnn_Whh, L1_gnn_bih, L1_gnn_bhh, L1_ffn_Wr, L1_ffn_br, L1_ffn_W1, L1_ffn_b1, L1_ffn_W2, L1_ffn_b2, L1_ffn_gamma, L1_ffn_beta):
    import jax
    import jax.numpy as jnp

    def _L0_gnn_ref(features, A, W1, b1, g1, be1, W2, b2, g2, be2):
        import jax, jax.numpy as jnp
        import numpy as np
        EPS = 1e-05

        def _batchnorm(x, gamma, beta):
            mu = jnp.mean(x, axis=0)
            var = jnp.var(x, axis=0)
            return (x - mu) * jax.lax.rsqrt(var + EPS) * gamma + beta
        b, n, d = features.shape
        A_norm = A + jnp.eye(n, dtype=A.dtype)
        deg = jnp.sum(A_norm, axis=0) + jnp.sum(A_norm, axis=1) - jnp.diagonal(A_norm)
        dinv = jax.lax.rsqrt(deg)
        A_hat = A_norm * dinv[:, None] * dinv[None, :]
        agg = jnp.einsum('nm,bmd->bnd', A_hat, features)
        x = agg.reshape(-1, d)
        h = jax.nn.relu(_batchnorm(x @ W1.T + b1, g1, be1))
        out = h @ W2.T + b2
        out = _batchnorm(out, g2, be2)
        return out.reshape(b, n, -1)

    def _L0_ffn_ref(x, Wg, bg, W1, b1, W2, b2):
        import jax, jax.numpy as jnp
        import numpy as np
        B, S, D, H, E, K = (8, 4096, 128, 512, 8, 2)
        gate_scores = jnp.einsum('bsd,ed->bse', x, Wg) + bg
        topk_scores, topk_idx = jax.lax.top_k(gate_scores, K)
        topk_probs = jax.nn.softmax(topk_scores, axis=-1)
        combine = jnp.sum(topk_probs[..., None] * jax.nn.one_hot(topk_idx, E, dtype=x.dtype), axis=-2)
        out = jnp.zeros_like(x)
        for e in range(E):
            h = jax.nn.relu(jnp.einsum('bsd,hd->bsh', x, W1[e]) + b1[e])
            y = jnp.einsum('bsh,dh->bsd', h, W2[e]) + b2[e]
            out = out + combine[..., e:e + 1] * y
        return out

    def _L1_gnn_ref(x, adj, Wg0, bg0, Wg1, bg1, Wih, Whh, bih, bhh):
        import jax, jax.numpy as jnp
        import numpy as np
        B, T, D, H = (64, 1024, 128, 128)
        MAX_SKIP = 4

        def _lstm_last(Wih, Whh, bih, bhh, xs):
            N, _, Hd = xs.shape
            bias = bih + bhh

            def step(carry, x_t):
                h, c = carry
                g = x_t @ Wih.T + h @ Whh.T + bias
                i, f, gg, o = jnp.split(g, 4, axis=-1)
                c = jax.nn.sigmoid(f) * c + jax.nn.sigmoid(i) * jnp.tanh(gg)
                h = jax.nn.sigmoid(o) * jnp.tanh(c)
                return ((h, c), None)
            init = (jnp.zeros((N, Hd), xs.dtype), jnp.zeros((N, Hd), xs.dtype))
            (h_last, _), _ = jax.lax.scan(step, init, jnp.swapaxes(xs, 0, 1))
            return h_last
        h = jax.nn.relu(jnp.einsum('ts,bsh->bth', adj, x @ Wg0 + bg0))
        h = jax.nn.relu(jnp.einsum('ts,bsh->bth', adj, h @ Wg1 + bg1))
        Bv, Tv, Hd = h.shape
        for p in range(1, MAX_SKIP + 1):
            nw = Tv // p
            wins = h[:, :nw * p, :].reshape(Bv * nw, p, Hd)
            last = _lstm_last(Wih[p - 1], Whh[p - 1], bih[p - 1], bhh[p - 1], wins)
            idx = jnp.arange(nw) * p + (p - 1)
            h = h.at[:, idx, :].set(last.reshape(Bv, nw, Hd))
        return h

    def _L1_ffn_ref(x, Wr, br, W1, b1, W2, b2, gamma, beta):
        import math
        import jax, jax.numpy as jnp
        import numpy as np
        CAPACITY_FACTOR = 1.25
        TOP_K = 2
        LN_EPS = 1e-05

        def _layer_norm(x, gamma, beta):
            mu = jnp.mean(x, axis=-1, keepdims=True)
            var = jnp.var(x, axis=-1, keepdims=True)
            return (x - mu) * jax.lax.rsqrt(var + LN_EPS) * gamma + beta
        B, S, D = x.shape
        E = Wr.shape[1]
        N = B * S
        K = TOP_K
        logits = jnp.mean(x, axis=1) @ Wr + br
        routing_weights = jax.nn.softmax(logits, axis=-1)
        capacity = float(math.ceil(N * CAPACITY_FACTOR / E))
        expected_loads = routing_weights.sum(axis=0) * (N / B)
        scale = jnp.where(expected_loads > capacity, capacity / expected_loads, 1.0)
        routing_weights = jax.nn.softmax(routing_weights * scale, axis=-1)
        rw_tok = jnp.broadcast_to(routing_weights[:, None, :], (B, S, E)).reshape(N, E)
        top_w, top_i = jax.lax.top_k(rw_tok, K)
        top_w = jax.nn.softmax(top_w, axis=-1)
        xf = x.reshape(N, D)
        h = jax.nn.gelu(jnp.einsum('nd,edf->enf', xf, W1) + b1[:, None, :], approximate=False)
        y = jnp.einsum('enf,efd->end', h, W2) + b2[:, None, :]
        w_dense = jnp.zeros((N, E), x.dtype).at[jnp.arange(N)[:, None], top_i].add(top_w)
        out = jnp.einsum('ne,end->nd', w_dense, y).reshape(B, S, D)
        out = _layer_norm(out + x, gamma, beta)
        return out
    x = x + _L0_gnn_ref(_layernorm(x, axis=-1), adj, L0_gnn_W1, L0_gnn_b1, L0_gnn_g1, L0_gnn_be1, L0_gnn_W2, L0_gnn_b2, L0_gnn_g2, L0_gnn_be2)
    x = x + _L0_ffn_ref(_layernorm(x, axis=-1), L0_ffn_Wg, L0_ffn_bg, L0_ffn_W1, L0_ffn_b1, L0_ffn_W2, L0_ffn_b2)
    x = x + _L1_gnn_ref(_layernorm(x, axis=-1), adj, L1_gnn_Wg0, L1_gnn_bg0, L1_gnn_Wg1, L1_gnn_bg1, L1_gnn_Wih, L1_gnn_Whh, L1_gnn_bih, L1_gnn_bhh)
    x = x + _L1_ffn_ref(_layernorm(x, axis=-1), L1_ffn_Wr, L1_ffn_br, L1_ffn_W1, L1_ffn_b1, L1_ffn_W2, L1_ffn_b2, L1_ffn_gamma, L1_ffn_beta)
    return x

_drawn_inputs = setup_inputs


def setup_inputs(seed=0):
    import zlib

    import numpy as np

    out = dict(_drawn_inputs(seed))
    spreads = {'L0_gnn_b1': (0.0, 2.0),
     'L0_gnn_g1': (1.0, 0.2),
     'L0_gnn_be1': (0.0, 0.1),
     'L0_gnn_b2': (0.0, 2.0),
     'L0_gnn_g2': (1.0, 0.2),
     'L0_gnn_be2': (0.0, 0.1),
     'L1_gnn_bg0': (0.0, 0.631),
     'L1_gnn_bg1': (0.0, 0.1),
     'L1_ffn_br': (0.0, 0.1),
     'L1_ffn_b1': (0.0, 0.431),
     'L1_ffn_b2': (0.0, 0.3),
     'L1_ffn_gamma': (1.0, 0.2),
     'L1_ffn_beta': (0.0, 0.1)}
    factors = {'L0_ffn_b1': 5.334, 'L1_gnn_bhh': 4.056, 'L0_ffn_b2': 4.274}
    for name, (base, spread) in spreads.items():
        noise = np.random.default_rng([zlib.crc32(name.encode()), seed]).standard_normal(out[name].shape)
        drawn = base * np.exp(spread * noise) if base else spread * noise
        out[name] = jnp.asarray(drawn.astype(out[name].dtype))
    for name, factor in factors.items():
        out[name] = (out[name] * factor).astype(out[name].dtype)
    return out
```

```python
from contextlib import ExitStack

import concourse.bass as bass
from concourse import mybir

F32 = mybir.dt.float32
F32R = mybir.dt.float32r
I32 = mybir.dt.int32
ALU = mybir.AluOpType
ACT = mybir.ActivationFunctionType
AX = mybir.AxisListType

P = 128
B, S, D = 16, 512, 128
T = B
N = S
K = S // P
TOK = B * S
H1 = 256
C1 = H1 // P
E = 8
FH = 512
FJ = FH // P
GH = 256
GJ = GH // P
EW = 2 * GH
EPS = 1e-5
BIG = 3.0e38
NG = 4
CAP = float(-(-(TOK * 5) // (4 * E)))

VEC = {}
_at = 0
for _name, _n in (("gb1", C1), ("gg1", C1), ("gbe1", C1), ("gb2", 1), ("gg2", 1), ("gbe2", 1),
                  ("fb1", E * FJ), ("fb2", E), ("bih", 4 * NG), ("bhh", 4 * NG), ("hb1", E * GJ),
                  ("gamma", 1), ("beta", 1)):
    VEC[_name] = (_at, _at + _n)
    _at += _n
NVEC = _at


def staggered(eng, n, parts):
    edge = max(2, -(-max(lag for _, lag in parts) // 2) * 2)
    for t in range(edge):
        for fn, lag in parts:
            if t >= lag:
                fn(t - lag, (t - lag) % 2)
    with eng.Fori(edge // 2, n // 2) as i:
        for u in range(2):
            for fn, lag in parts:
                fn(i * 2 + (u - lag), (u - lag) % 2)
    for t in range(n, n + max(lag for _, lag in parts)):
        for fn, lag in parts:
            if t - lag < n:
                fn(t - lag, (t - lag) % 2)


def cols(t, n=N, off=0):
    return bass.ds(t * n + off, n)



class Stage(ExitStack):

    def __init__(self):
        super().__init__()
        self.used = []

    def semaphore(self, nc, name):
        self.used.append(self.enter_context(nc.semaphore(name)))
        return self.used[-1]

    def block(self, nc):
        self.callback(self.clear, nc)
        return self.enter_context(nc.Block())

    def clear(self, nc):
        numbers = sorted(s.num for s in self.used)
        with nc.Block() as block:
            @block.gpsimd
            def _(pool):
                first = last = numbers[0]
                for n in numbers[1:] + [None]:
                    if n != last + 1:
                        pool.sem_clear(range(first, last + 1))
                        first = n
                    last = n


class Norm:

    def __init__(self, nc, ctx, name, ps, ident, epst):
        self.nc, self.ps, self.ident, self.epst = nc, ps, ident, epst

        def sb(n, s):
            return ctx.enter_context(nc.sbuf_tensor(f"{name}_{n}", s, F32))

        def sem(n):
            return ctx.semaphore(nc, f"{name}_{n}")

        self.src = sb("src", [P, 2, N])
        self.stats = sb("stats", [P, 2, K, 6])
        self.mv = sb("mv", [P, 2, K, 2])
        self.sd = sb("sd", [P, 2, K])
        self.rs = sb("rs", [P, 2, K])
        self.nmr = sb("nmr", [P, 2, K])
        self.xt = sb("xt", [P, 2, K, P])
        self.src_ready = sem("src_ready")
        self.open = sem("open")
        self.turned = sem("turned")
        self.stats_done = sem("stats_done")
        self.mv_done = sem("mv_done")
        self.sd_done = sem("sd_done")
        self.rs_done = sem("rs_done")
        self.nmr_done = sem("nmr_done")
        self.normed = sem("normed")
        self.back = sem("back")
        self.out_free = sem("out_free")

    def turn(self, pe):
        def fn(t, u):
            pe.wait_ge(self.src_ready, t + 3)
            pe.wait_ge(self.normed, t + 1)
            for k in range(K):
                ins = pe.transpose(self.ps[u][:, k * P:(k + 1) * P],
                                   self.src[:, u, k * P:(k + 1) * P], self.ident[:, :])
            ins.then_inc(self.turned, 1)
        return fn

    def turn_back(self, pe):
        def fn(t, u):
            pe.wait_ge(self.normed, t + 3)
            pe.wait_ge(self.out_free, t + 1)
            for k in range(K):
                ins = pe.transpose(self.ps[2 + u][:, k * P:(k + 1) * P], self.xt[:, u, k, :],
                                   self.ident[:, :])
            ins.then_inc(self.back, 1)
        return fn

    def moments(self, dve):
        def fn(t, u):
            dve.wait_ge(self.turned, t + 3)
            for k in range(K):
                ins = dve.bn_stats(self.stats[:, u, k, :], self.ps[u][:, k * P:(k + 1) * P])
            ins.then_inc(self.stats_done, 1)
            dve.wait_ge(self.open, 1)
            dve.wait_ge(self.stats_done, t + 1)
            for k in range(K):
                ins = dve.bn_aggr(self.mv[:, u, k, :], self.stats[:, u, k, :])
            ins.then_inc(self.mv_done, 1)
        return fn

    def scales(self, dve):
        def fn(t, u):
            dve.wait_ge(self.sd_done, t + 1)
            dve.reciprocal(self.rs[:, u, :], self.sd[:, u, :]).then_inc(self.rs_done, 1)
            dve.wait_ge(self.rs_done, t + 1)
            dve.scalar_tensor_tensor(self.nmr[:, u, :], self.mv[:, u, :, 0], -1.0, self.rs[:, u, :],
                                     ALU.mult, ALU.mult).then_inc(self.nmr_done, 1)
        return fn

    def deviations(self, act):
        def fn(t, u):
            act.wait_ge(self.mv_done, t + 1)
            act.activation(self.sd[:, u, :], self.mv[:, u, :, 1], ACT.Sqrt,
                           bias=self.epst[:, 0:1]).then_inc(self.sd_done, 1)
        return fn

    def scale(self, act):
        def fn(t, u):
            act.wait_ge(self.nmr_done, t + 1)
            act.wait_ge(self.back, t + 1)
            for k in range(K):
                ins = act.activation(self.xt[:, u, k, :], self.ps[u][:, k * P:(k + 1) * P],
                                     ACT.Identity, bias=self.nmr[:, u, k:k + 1],
                                     scale=self.rs[:, u, k:k + 1])
            ins.then_inc(self.normed, 1)
        return fn

    def wait_out(self, eng, t):
        eng.wait_ge(self.back, t + 3)

    def wait_src(self, eng, t):
        eng.wait_ge(self.turned, t + 1)


def prepare(nc, ps, d, res):
    with Stage() as ctx:
        def sb(n, s, dt=F32):
            return ctx.enter_context(nc.sbuf_tensor(f"p_{n}", s, dt))

        def sem(n):
            return ctx.semaphore(nc, f"p_{n}")

        anat = sb("anat", [P, K, N])
        at = sb("at", [P, K, N])
        raw = sb("raw", [P, H1 + C1 * P])
        scr = sb("scr", [P, K, P])
        diag4 = sb("diag4", [P, K, P])
        ones = sb("ones", [P, P])
        ahat = sb("ahat", [P, K, N])
        rsum = sb("rsum", [P, K])
        csum = sb("csum", [P, K])
        dia = sb("dia", [P, K])
        deg1 = sb("deg1", [P, K])
        deg = sb("deg", [P, K])
        sdeg = sb("sdeg", [P, K])
        dinv = sb("dinv", [P, K])
        st = sb("st", [P, B * K, 6])
        mv = sb("mv", [P, B * K, 2])
        sd = sb("sd", [P, B * K])
        ident, epst = res.ident, res.epst
        cst, idn, xin, ain, win, vin = (sem(n) for n in ("cst", "idn", "xin", "ain", "win", "vin"))
        plus = sem("plus")
        sums = sem("sums")
        degs = sem("degs")
        sdegs = sem("sdegs")
        dinvs = sem("dinvs")
        diags = sem("diags")
        dbc = sem("dbc")
        ah = sem("ah")
        hi = sem("hi")
        lo = sem("lo")
        stt = sem("stt")
        mvs = sem("mvs")
        sds = sem("sds")
        rss = sem("rss")
        block = ctx.block(nc)

        @block.sync
        def _(sp):
            sp.dma_start(anat[:], d["adj"]).then_inc(ain, 16)
            sp.dma_start(at[:], d["adjT"]).then_inc(ain, 16)
            sp.dma_start(res.xt[:, 0:B * K // 2, :], d["x_tm"][:, 0:B * K // 2, :]).then_inc(xin, 16)
            sp.dma_start(res.xt[:, B * K // 2:, :], d["x_tm"][:, B * K // 2:, :]).then_inc(xin, 16)
            sp.dma_start(raw[:], d["gw"]).then_inc(win, 16)
            sp.dma_start(res.vec[:], d["vec"]).then_inc(vin, 16)
            sp.dma_start(res.X[:], d["x_fm"]).then_inc(vin, 16)
            sp.wait_ge(vin, 32)

        @block.gpsimd
        def _(pool):
            pool.memset(ident[:, :], 0.0).then_inc(idn, 1)
            pool.wait_ge(idn, 1)
            pool.affine_select(out=ident[:, :], in_=ident[:, :], compare_op=ALU.not_equal, fill=1.0,
                               base=0, pattern=[[-1, P]], channel_multiplier=1).then_inc(idn, 1)
            pool.memset(epst[:, :], EPS).then_inc(cst, 1)
            pool.memset(ones[:, :], 1.0).then_inc(cst, 1)

        @block.vector
        def _(dve):
            dve.wait_ge(ain, 32)
            dve.wait_ge(idn, 2)
            for k in range(K):
                for m in (anat, at):
                    blk = m[:, k, k * P:(k + 1) * P]
                    dve.tensor_tensor(blk, blk, ident[:, :], ALU.add).then_inc(plus, 1)
            dve.wait_ge(plus, 2 * K)
            dve.tensor_reduce(rsum[:, :], anat[:], AX.X, ALU.add).then_inc(sums, 1)
            dve.tensor_reduce(csum[:, :], at[:], AX.X, ALU.add).then_inc(sums, 1)
            for k in range(K):
                dve.tensor_tensor(scr[:, k, :], anat[:, k, k * P:(k + 1) * P], ident[:, :],
                                  ALU.mult).then_inc(sums, 1)
            dve.wait_ge(sums, 2 + K)
            dve.tensor_reduce(dia[:, :], scr[:], AX.X, ALU.add).then_inc(sums, 1)
            dve.tensor_tensor(deg1[:, :], rsum[:, :], csum[:, :], ALU.add).then_inc(sums, 1)
            dve.wait_ge(sums, 4 + K)
            dve.tensor_tensor(deg[:, :], deg1[:, :], dia[:, :], ALU.subtract).then_inc(degs, 1)
            dve.wait_ge(sdegs, 1)
            dve.reciprocal(dinv[:, :], sdeg[:, :]).then_inc(dinvs, 1)
            dve.wait_ge(dinvs, 1)
            for k in range(K):
                dve.tensor_scalar(diag4[:, k, :], ident[:, :], dinv[:, k:k + 1], None,
                                  ALU.mult).then_inc(diags, 1)
            dve.wait_ge(dbc, 1)
            for k in range(K):
                dve.scalar_tensor_tensor(ahat[:, k, :], at[:, k, :], dinv[:, k:k + 1], ps[0][:, :],
                                         ALU.mult, ALU.mult).then_inc(ah, 1)
            dve.wait_ge(hi, 1)
            dve.tensor_tensor(res.ahL[:], ahat[:], res.ahH[:].bitcast(F32), ALU.subtract).then_inc(lo, 1)
            dve.wait_ge(hi, 2)
            dve.tensor_tensor(res.gwL[:], raw[:], res.gwH[:].bitcast(F32), ALU.subtract).then_inc(lo, 1)
            dve.wait_ge(xin, 32)
            with dve.Fori(0, B) as b:
                for k in range(K):
                    dve.bn_stats(st[:, bass.ds(b * K + k, 1), :], res.xt[:, bass.ds(b * K + k, 1), :]).then_inc(stt, 1)
            dve.wait_ge(stt, B * K)
            for k in range(B * K):
                dve.bn_aggr(mv[:, k, :], st[:, k, :]).then_inc(mvs, 1)
            dve.wait_ge(sds, 1)
            dve.reciprocal(res.rs0[:, :], sd[:, :]).then_inc(rss, 1)
            dve.wait_ge(rss, 1)
            dve.wait_ge(mvs, B * K)
            dve.scalar_tensor_tensor(res.nmr0[:, :], mv[:, :, 0], -1.0, res.rs0[:, :],
                                     ALU.mult, ALU.mult).then_inc(rss, 1)

        @block.scalar
        def _(act):
            act.wait_ge(degs, 1)
            act.activation(sdeg[:, :], deg[:, :], ACT.Sqrt).then_inc(sdegs, 1)
            act.wait_ge(ah, K)
            act.activation(res.ahH[:], ahat[:], ACT.Copy).then_inc(hi, 1)
            act.wait_ge(win, 16)
            act.activation(res.gwH[:], raw[:], ACT.Copy).then_inc(hi, 1)
            act.wait_ge(cst, 2)
            act.wait_ge(mvs, B * K)
            act.activation(sd[:, :], mv[:, :, 1], ACT.Sqrt, bias=epst[:, 0:1]).then_inc(sds, 1)

        @block.tensor
        def _(pe):
            pe.wait_ge(cst, 2)
            pe.wait_ge(diags, K)
            for k in range(K):
                ins = pe.matmul(ps[0][:, k * P:(k + 1) * P], ones[:, :], diag4[:, k, :],
                                start=True, stop=True)
            ins.then_inc(dbc, 1)


def three(pe, out, hi, lo, rhi, rlo, start, stop):
    pe.matmul(out, lo, rhi, start=start, stop=False)
    pe.matmul(out, hi, rlo, start=False, stop=False)
    return pe.matmul(out, hi, rhi, start=False, stop=stop)


def first_graph(nc, ps, res, Y1):
    with Stage() as ctx:
        def sb(n, s, dt=F32):
            return ctx.enter_context(nc.sbuf_tensor(f"b_{n}", s, dt))

        def sem(n):
            return ctx.semaphore(nc, f"b_{n}")

        xn = sb("xn", [P, 2, K, P])
        xH = sb("xH", [P, 2, K, P], F32R)
        xL = sb("xL", [P, 2, K, P], F32R)
        gH = sb("gH", [P, 2, N], F32R)
        gL = sb("gL", [P, 2, N], F32R)
        normed, xh, xl = sem("normed"), sem("xh"), sem("xl")
        agg, gh, gl, y, yev, sts = (sem(n) for n in ("agg", "gh", "gl", "y", "yev", "sts"))
        block = ctx.block(nc)

        @block.scalar
        def _(act):
            act.sem_inc(gh, 2)
            act.sem_inc(yev, 2)

            def norm(t, u):
                act.wait_ge(xl, t + 1)
                for k in range(K):
                    ins = act.activation(xn[:, u, k, :], res.xt[:, bass.ds(t * K + k, 1), :],
                                         ACT.Identity, bias=res.nmr0[:, bass.ds(t * K + k, 1)],
                                         scale=res.rs0[:, bass.ds(t * K + k, 1)])
                ins.then_inc(normed, 1)
                act.wait_ge(normed, t + 1)
                act.wait_ge(agg, t + 1)
                act.activation(xH[:, u], xn[:, u], ACT.Copy).then_inc(xh, 1)

            def agg_hi(t, u):
                act.wait_ge(agg, t + 3)
                act.wait_ge(y, t + 1)
                act.activation(gH[:, u, :], ps[u][:, :], ACT.Copy).then_inc(gh, 1)

            def evac(t, u):
                act.wait_ge(y, t + 3)
                for c in range(C1):
                    ins = act.activation(Y1[:, c, cols(t)], ps[2 + 2 * u + c][:, :], ACT.Identity,
                                         bias=res.col("gb1", c))
                ins.then_inc(yev, 1)

            staggered(act, B, [(norm, 0), (agg_hi, 1), (evac, 2)])

        @block.vector
        def _(dve):
            dve.sem_inc(xl, 2)
            dve.sem_inc(gl, 2)

            def x_lo(t, u):
                dve.wait_ge(xh, t + 1)
                dve.wait_ge(agg, t + 1)
                dve.tensor_tensor(xL[:, u], xn[:, u], xH[:, u].bitcast(F32), ALU.subtract).then_inc(xl, 1)

            def agg_lo(t, u):
                dve.wait_ge(gh, t + 3)
                dve.wait_ge(y, t + 1)
                dve.tensor_tensor(gL[:, u, :], ps[u][:, :], gH[:, u, :].bitcast(F32),
                                  ALU.subtract).then_inc(gl, 1)

            def stats(t, u):
                dve.wait_ge(yev, t + 3)
                for c in range(C1):
                    ins = dve.bn_stats(res.st1[:, c, bass.ds(t, 1), :], Y1[:, c, cols(t)])
                ins.then_inc(sts, 1)

            staggered(dve, B, [(x_lo, 0), (agg_lo, 1), (stats, 2)])

        @block.tensor
        def _(pe):
            pe.sem_inc(agg, 2)
            pe.sem_inc(y, 2)

            def aggregate(t, u):
                pe.wait_ge(xl, t + 3)
                pe.wait_ge(gl, t + 1)
                for k in range(K):
                    ins = three(pe, ps[u][:, :], xH[:, u, k, :], xL[:, u, k, :], res.ahH[:, k, :],
                                res.ahL[:, k, :], k == 0, k == K - 1)
                ins.then_inc(agg, 1)

            def project(t, u):
                pe.wait_ge(gl, t + 3)
                pe.wait_ge(yev, t + 1)
                for c in range(C1):
                    ins = three(pe, ps[2 + 2 * u + c][:, :], res.gwH[:, c * P:(c + 1) * P],
                                res.gwL[:, c * P:(c + 1) * P], gH[:, u, :], gL[:, u, :], True, True)
                ins.then_inc(y, 1)

            staggered(pe, B, [(aggregate, 0), (project, 1)])


def batch_norm_scales(dve, act, sems, stats, c_n, mv, sd, rs, s, t, gamma, beta, epst, role):
    aggd, sdd, rsd, sdone, tmp, ready = sems
    if role == "dve":
        for c in range(c_n):
            dve.bn_aggr(mv[:, c, :], stats[:, c]).then_inc(aggd, 1)
        dve.wait_ge(sdd, 1)
        dve.reciprocal(rs[:, :], sd[:, :]).then_inc(rsd, 1)
        dve.wait_ge(rsd, 1)
        dve.tensor_tensor(s[:, :], rs[:, :], gamma, ALU.mult).then_inc(sdone, 1)
        dve.wait_ge(sdone, 1)
        dve.tensor_tensor(rs[:, :], mv[:, :, 0], s[:, :], ALU.mult).then_inc(tmp, 1)
        dve.wait_ge(tmp, 1)
        dve.tensor_tensor(t[:, :], beta, rs[:, :], ALU.subtract).then_inc(ready, 1)
    else:
        act.wait_ge(aggd, c_n)
        act.activation(sd[:, :], mv[:, :, 1], ACT.Sqrt, bias=epst[:, 0:1]).then_inc(sdd, 1)


def second_graph(nc, ps, res, Y1, Y2):
    with Stage() as ctx:
        def sb(n, s, dt=F32):
            return ctx.enter_context(nc.sbuf_tensor(f"c_{n}", s, dt))

        def sem(n):
            return ctx.semaphore(nc, f"c_{n}")

        mv, sd, rs = sb("mv", [P, C1, 2]), sb("sd", [P, C1]), sb("rs", [P, C1])
        s1, t1 = sb("s1", [P, C1]), sb("t1", [P, C1])
        h = sb("h", [P, 2, C1, N])
        hH = sb("hH", [P, 2, C1, N], F32R)
        hL = sb("hL", [P, 2, C1, N], F32R)
        bn = [sem(n) for n in ("bn_aggr", "bn_sd", "bn_rs", "bn_s", "bn_ms", "bn_ready")]
        hf, hh, hl, y, yev, sts = (sem(n) for n in ("hf", "hh", "hl", "y", "yev", "sts"))
        block = ctx.block(nc)

        @block.scalar
        def _(act):
            act.sem_inc(yev, 2)
            batch_norm_scales(None, act, bn, res.st1, C1, mv, sd, rs, s1, t1, res.cols("gg1"),
                              res.cols("gbe1"), res.epst, "act")
            act.wait_ge(bn[5], 1)

            def hidden(t, u):
                act.wait_ge(hl, t + 1)
                for c in range(C1):
                    ins = act.activation(h[:, u, c, :], Y1[:, c, cols(t)], ACT.Relu,
                                         bias=t1[:, c:c + 1], scale=s1[:, c:c + 1])
                ins.then_inc(hf, 1)

            def evac(t, u):
                act.wait_ge(y, t + 3)
                act.activation(Y2[:, cols(t)], ps[u][:, :], ACT.Identity,
                               bias=res.col("gb2", 0)).then_inc(yev, 1)

            staggered(act, B, [(hidden, 0), (evac, 2)])

        @block.vector
        def _(dve):
            dve.sem_inc(hl, 2)
            batch_norm_scales(dve, None, bn, res.st1, C1, mv, sd, rs, s1, t1, res.cols("gg1"),
                              res.cols("gbe1"), res.epst, "dve")

            def parts(t, u):
                dve.wait_ge(hf, t + 1)
                dve.wait_ge(y, t + 1)
                dve.tensor_copy(hH[:, u], h[:, u]).then_inc(hh, 1)
                dve.wait_ge(hh, t + 1)
                dve.tensor_tensor(hL[:, u], h[:, u], hH[:, u].bitcast(F32), ALU.subtract).then_inc(hl, 1)

            def stats(t, u):
                dve.wait_ge(yev, t + 3)
                dve.bn_stats(res.st2[:, 0, bass.ds(t, 1), :], Y2[:, cols(t)]).then_inc(sts, 1)

            staggered(dve, B, [(parts, 0), (stats, 2)])

        @block.tensor
        def _(pe):
            pe.sem_inc(y, 2)

            def project(t, u):
                pe.wait_ge(hl, t + 3)
                pe.wait_ge(yev, t + 1)
                for c in range(C1):
                    o = H1 + c * P
                    ins = three(pe, ps[u][:, :], res.gwH[:, o:o + P], res.gwL[:, o:o + P],
                                hH[:, u, c, :], hL[:, u, c, :], c == 0, c == C1 - 1)
                ins.then_inc(y, 1)

            staggered(pe, B, [(project, 0)])


def gate_stage(nc, ps, res, Y, fwH, fwL, d, scratch):
    with Stage() as ctx:
        def sb(n, s, dt=F32):
            return ctx.enter_context(nc.sbuf_tensor(f"d_{n}", s, dt))

        def sem(n):
            return ctx.semaphore(nc, f"d_{n}")

        ln = Norm(nc, ctx, "dln", ps, res.ident, res.epst)
        mv, sd, rs = sb("mv", [P, 1, 2]), sb("sd", [P, 1]), sb("rs", [P, 1])
        s2, t2 = sb("s2", [P, 1]), sb("t2", [P, 1])
        tmp = sb("tmp", [P, 2, N])
        xg = sb("xg", [P, 2, N])
        wg = sb("wg", [P, E])
        raw = sb("raw", [P, 2, N])
        bg = sb("bg", [P, E])
        rank = sb("rank", [P, E])
        G = B * K
        sc, eq, o1, o2 = (sb(n, [P, G, E]) for n in ("sc", "eq", "o1", "o2"))
        m1, m2, mx, ex, den, p1, p2 = (sb(n, [P, G]) for n in ("m1", "m2", "mx", "ex", "den", "p1", "p2"))
        ct = sb("ct", [P, N])
        bn = [sem(n) for n in ("bn_aggr", "bn_sd", "bn_rs", "bn_s", "bn_ms", "bn_ready")]
        tmpd, xgd, xnd, gated, copied, win, gin, whi, wlo, rk = (sem(n) for n in (
            "tmpd", "xgd", "xnd", "gated", "copied", "win", "gin", "whi", "wlo", "rk"))
        step, exd, ctd, ctev, sto = (sem(n) for n in ("step", "exd", "ctd", "ctev", "sto"))
        block = ctx.block(nc)
        pieces = 2 * E * FH // N

        @block.sync
        def _(sp):
            sp.dma_start(wg[:], d["wg"]).then_inc(gin, 16)
            sp.dma_start(bg[:], d["bg"][0].partition_broadcast(P)).then_inc(gin, 16)
            for t in range(pieces):
                if t >= 2:
                    sp.wait_ge(wlo, t - 1)
                sp.dma_start(raw[:, t % 2, :], d["fw"][:, t * N:(t + 1) * N]).then_inc(win, 16)
                sp.wait_ge(win, 16 * (t + 1))
            sp.wait_ge(ctev, 1)
            sp.dma_start(scratch.rearrange("q r n -> r q n"),
                         ct[:].rearrange("r (q n) -> r q n", n=P)).then_inc(sto, 16)
            sp.wait_ge(sto, 16)

        @block.gpsimd
        def _(pool):
            for e in range(E):
                pool.memset(rank[:, e:e + 1], float(E - e)).then_inc(rk, 1)
            pool.sem_inc(copied, 2)

            def keep_x(t, u):
                pool.wait_ge(ln.src_ready, t + 3)
                pool.tensor_copy(res.X[:, cols(t)], ln.src[:, u, :]).then_inc(copied, 1)

            def weights(t, u):
                pool.wait_ge(win, t * 16 + 16)
                pool.tensor_copy(fwH[:, cols(t)], raw[:, u, :]).then_inc(whi, 1)
                pool.wait_ge(whi, t + 1)
                pool.tensor_tensor(fwL[:, cols(t)], raw[:, u, :], fwH[:, cols(t)].bitcast(F32),
                                   ALU.subtract).then_inc(wlo, 1)

            staggered(pool, B, [(keep_x, 0), (weights, 0)])

        @block.scalar
        def _(act):
            act.sem_inc(ln.normed, 2)
            act.sem_inc(ln.out_free, 2)
            batch_norm_scales(None, act, bn, res.st2, 1, mv, sd, rs, s2, t2, None, None, res.epst, "act")
            act.wait_ge(bn[5], 1)

            def normed(t, u):
                act.wait_ge(ln.src_ready, t + 1)
                act.activation(tmp[:, u, :], Y[:, cols(t)], ACT.Identity, bias=t2[:, 0:1],
                               scale=s2[:, 0:1]).then_inc(tmpd, 1)

            def evac(t, u):
                ln.wait_out(act, t)
                act.wait_ge(gated, t + 1)
                act.wait_ge(xnd, t + 1)
                act.activation(xg[:, u, :], ps[2 + u][:, :], ACT.Copy).then_inc(ln.out_free, 1)

            staggered(act, B, [(normed, 0), (ln.deviations(act), 1), (evac, 2), (ln.scale(act), 1)])
            act.wait_ge(step, 11)
            act.activation(ex[:, :], den[:, :], ACT.Exp).then_inc(exd, 1)
            act.wait_ge(ctd, 1)
            act.activation(ct[:, :], ps[5][:, :], ACT.Copy).then_inc(ctev, 1)

        @block.vector
        def _(dve):
            dve.sem_inc(ln.open, 1)
            dve.sem_inc(ln.src_ready, 2)
            dve.sem_inc(xnd, 2)
            batch_norm_scales(dve, None, bn, res.st2, 1, mv, sd, rs, s2, t2, res.cols("gg2"),
                              res.cols("gbe2"), res.epst, "dve")

            def add(t, u):
                dve.wait_ge(tmpd, t + 1)
                ln.wait_src(dve, t)
                dve.wait_ge(copied, t + 1)
                dve.tensor_tensor(ln.src[:, u, :], tmp[:, u, :], res.X[:, cols(t)],
                                  ALU.add).then_inc(ln.src_ready, 1)

            def store(t, u):
                dve.wait_ge(ln.out_free, t + 3)
                dve.tensor_copy(Y[:, cols(t)], xg[:, u, :]).then_inc(xnd, 1)

            staggered(dve, B, [(add, 0), (ln.moments(dve), 1), (store, 2), (ln.scales(dve), 1)])

            done = [0]

            def then(ins):
                ins.then_inc(step, 1)
                done[0] += 1
                dve.wait_ge(step, done[0])

            def wide(a):
                return a.unsqueeze(2).to_broadcast([P, G, E])

            def over(a):
                return a.unsqueeze(1).to_broadcast([P, G, E])

            dve.wait_ge(gin, 32)
            dve.wait_ge(rk, E)
            dve.wait_ge(gated, B + 2)
            then(dve.tensor_tensor(sc[:], ps[4][:].rearrange("p (g e) -> p g e", e=E), over(bg[:]), ALU.add))
            then(dve.tensor_reduce(m1[:], sc[:], AX.X, ALU.max))
            then(dve.tensor_tensor(eq[:], sc[:], wide(m1[:]), ALU.is_equal))
            then(dve.tensor_tensor(eq[:], eq[:], over(rank[:]), ALU.mult))
            then(dve.tensor_reduce(mx[:], eq[:], AX.X, ALU.max))
            then(dve.tensor_tensor(o1[:], eq[:], wide(mx[:]), ALU.is_equal))
            then(dve.scalar_tensor_tensor(sc[:], o1[:], -BIG, sc[:], ALU.mult, ALU.add))
            then(dve.tensor_reduce(m2[:], sc[:], AX.X, ALU.max))
            then(dve.tensor_tensor(eq[:], sc[:], wide(m2[:]), ALU.is_equal))
            then(dve.tensor_tensor(eq[:], eq[:], over(rank[:]), ALU.mult))
            then(dve.tensor_tensor(den[:], m2[:], m1[:], ALU.subtract))
            then(dve.tensor_reduce(mx[:], eq[:], AX.X, ALU.max))
            then(dve.tensor_tensor(o2[:], eq[:], wide(mx[:]), ALU.is_equal))
            dve.wait_ge(exd, 1)
            then(dve.tensor_scalar(den[:], ex[:], 1.0, None, ALU.add))
            then(dve.reciprocal(p1[:], den[:]))
            then(dve.tensor_tensor(p2[:], ex[:], p1[:], ALU.mult))
            then(dve.tensor_tensor(o1[:], o1[:], wide(p1[:]), ALU.mult))
            then(dve.tensor_tensor(o2[:], o2[:], wide(p2[:]), ALU.mult))
            then(dve.tensor_tensor(sc[:], o1[:], o2[:], ALU.add))

        @block.tensor
        def _(pe):
            pe.sem_inc(ln.turned, 2)
            pe.sem_inc(ln.back, 2)
            pe.sem_inc(gated, 2)
            pe.wait_ge(gin, 32)

            def gate(t, u):
                pe.wait_ge(ln.out_free, t + 3)
                for k in range(K):
                    ins = pe.matmul(ps[4][:, bass.ds((t * K + k) * E, E)], xg[:, u, k * P:(k + 1) * P],
                                    wg[:, :], start=True, stop=True)
                ins.then_inc(gated, 1)

            staggered(pe, B, [(ln.turn(pe), 0), (ln.turn_back(pe), 1), (gate, 2)])
            pe.wait_ge(step, 19)
            flat = sc[:].rearrange("p g e -> p (g e)")
            for q in range(K):
                ins = pe.transpose(ps[5][:, q * P:(q + 1) * P], flat[:, q * P:(q + 1) * P], res.ident[:, :])
            ins.then_inc(ctd, 1)


def experts(nc, ps, res, Y, fwH, fwL, scratch):
    Q = E * FJ
    R = 4
    with Stage() as ctx:
        def sb(n, s, dt=F32):
            return ctx.enter_context(nc.sbuf_tensor(f"e_{n}", s, dt))

        def sem(n):
            return ctx.semaphore(nc, f"e_{n}")

        xH, xL = sb("xH", [P, 2, N], F32R), sb("xL", [P, 2, N], F32R)
        hf = sb("hf", [P, 2, N])
        hH, hL = sb("hH", [P, R, N], F32R), sb("hL", [P, R, N], F32R)
        cb = sb("cb", [P, 2, K, E, P])
        tmp = sb("tmp", [P, 2, N])
        acc = sb("acc", [P, N])
        xh, xl = sem("x_high"), sem("x_low")
        m1, m2 = sem("hidden_sums"), sem("hidden_used")
        hfd, hha, hhd, lod = sem("hidden"), sem("high_act"), sem("high_dve"), sem("low")
        yrd, xadd, cbl, folded = sem("y_read"), sem("added"), sem("weights_in"), sem("folded")
        block = ctx.block(nc)
        cdram = scratch.rearrange("q (g e) n -> (q g) (e n)", e=E)

        @block.sync
        def _(sp):
            def load(t):
                sp.dma_start(cb[:, bass.ds(t % 2, 1)].rearrange("p o k e n -> p (o k e n)"),
                             cdram[bass.ds(t * K, K), :].rearrange("a m -> (a m)").partition_broadcast(P))\
                    .then_inc(cbl, 16)
                sp.wait_ge(cbl, t * 16 + 16)
            for t in range(B):
                if t >= 2:
                    sp.wait_ge(yrd, (t - 1) * E + 2)
                load(t)

        @block.gpsimd
        def _(pool):
            pool.sem_inc(xadd, 2)
            with pool.Fori(0, B) as t:
                for e in range(1, E):
                    pool.wait_ge(yrd, t * E + (e + 3))
                    if e == 1:
                        pool.wait_ge(folded, t + 1)
                    else:
                        pool.wait_ge(xadd, t * (E - 1) + (e + 1))
                    pool.tensor_tensor(acc[:, :], tmp[:, 0, :] if e == 1 else acc[:, :], tmp[:, e % 2, :],
                                       ALU.add).then_inc(xadd, 1)

        @block.scalar
        def _(act):
            act.sem_inc(hfd, R)
            act.sem_inc(hha, FJ - 1)
            with act.Fori(0, B) as t:
                for q in range(Q):
                    c = t * Q + q
                    e, j = q // FJ, q % FJ
                    act.wait_ge(m1, c + 1)
                    act.wait_ge(lod, c + 1)
                    ins = act.activation(hf[:, q % 2, :], ps[q % R][:, :], ACT.Relu,
                                         bias=res.col("fb1", q))
                    ins.then_inc(hfd, 1)
                    if j < FJ - 1:
                        act.wait_ge(m2, c + 1)
                        act.activation(hH[:, q % R, :], ps[q % R][:, :], ACT.Relu,
                                       bias=res.col("fb1", q)).then_inc(hha, 1)

        @block.vector
        def _(dve):
            dve.sem_inc(lod, 2)
            dve.sem_inc(yrd, 2)
            dve.sem_inc(folded, 1)

            def split_x(t):
                dve.tensor_copy(xH[:, bass.ds(t % 2, 1), :], Y[:, cols(t)].unsqueeze(1)).then_inc(xh, 1)
                dve.wait_ge(xh, t + 1)
                dve.tensor_tensor(xL[:, bass.ds(t % 2, 1), :], Y[:, cols(t)].unsqueeze(1),
                                  xH[:, bass.ds(t % 2, 1), :].bitcast(F32), ALU.subtract).then_inc(xl, 1)

            def weigh(t, e):
                dve.wait_ge(m2, t * Q + (e * FJ + FJ + R))
                dve.wait_ge(cbl, t * 16 + 16)
                dve.wait_ge(xadd, t * (E - 1) + (1, 2, 3, 3, 4, 5, 6, 7)[e])
                dve.scalar_tensor_tensor(tmp[:, e % 2, :].rearrange("p (k n) -> p k n", n=P),
                                         ps[4 + e % 2][:, :].rearrange("p (k n) -> p k n", n=P),
                                         res.col("fb2", e),
                                         cb[:, bass.ds(t % 2, 1), :, e, :].rearrange("p o k n -> p (o k) n"),
                                         ALU.add, ALU.mult).then_inc(yrd, 1)

            def fold(t):
                dve.wait_ge(xadd, t * (E - 1) + (E + 1))
                dve.tensor_tensor(res.X[:, cols(t)], res.X[:, cols(t)], acc[:, :], ALU.add)\
                    .then_inc(folded, 1)

            def body(t, first=False, last=False):
                for q in range(Q):
                    c = t * Q + q
                    e, j = q // FJ, q % FJ
                    dve.wait_ge(hfd, c + 1 + R)
                    dve.wait_ge(m2, c + 1)
                    if j == FJ - 1:
                        dve.tensor_copy(hH[:, q % R, :], hf[:, q % 2, :]).then_inc(hhd, 1)
                        dve.wait_ge(hhd, t * E + (e + 1))
                    else:
                        dve.wait_ge(hha, (t * E + e) * (FJ - 1) + (j + FJ))
                    dve.tensor_tensor(hL[:, q % R, :], hf[:, q % 2, :], hH[:, q % R, :].bitcast(F32),
                                      ALU.subtract).then_inc(lod, 1)
                    if j == 2 and (e or not first):
                        weigh(t if e else t - 1, (e - 1) % E)
                    if q == FJ + 1 and not first:
                        fold(t - 1)
                    if q == Q // 2 and not last:
                        if not first:
                            dve.wait_ge(m1, t * Q)
                        split_x(t + 1)

            split_x(0)
            body(0, first=True)
            with dve.Fori(1, B - 1) as t:
                body(t)
            body(B - 1, last=True)
            weigh(B - 1, E - 1)
            fold(B - 1)

        @block.tensor
        def _(pe):
            pe.sem_inc(m2, R)

            def first(t, q):
                c = t * Q + q
                if q == 0:
                    pe.wait_ge(xl, t + 1)
                if q % FJ < FJ - 1:
                    pe.wait_ge(hha, (t * E + q // FJ) * (FJ - 1) + (q % FJ + 1))
                else:
                    pe.wait_ge(hfd, c + 1)
                w = slice(q * P, (q + 1) * P)
                x = (xH[:, bass.ds(t % 2, 1), :], xL[:, bass.ds(t % 2, 1), :])
                three(pe, ps[q % R][:, :].unsqueeze(1), fwH[:, w], fwL[:, w], *x, True, True).then_inc(m1, 1)

            def second(t, q):
                e, j = q // FJ, q % FJ
                pe.wait_ge(lod, t * Q + (q + 3))
                if j == 0:
                    pe.wait_ge(yrd, t * E + (e + 1))
                w = slice((Q + q) * P, (Q + q + 1) * P)
                ins = three(pe, ps[4 + e % 2][:, :], fwH[:, w], fwL[:, w], hH[:, q % R, :], hL[:, q % R, :],
                            j == 0, j == FJ - 1)
                ins.then_inc(m2, 1)

            def body(t, last=False):
                for q in range(Q):
                    if q + 2 < Q:
                        first(t, q + 2)
                    elif not last:
                        first(t + 1, q + 2 - Q)
                    second(t, q)

            first(0, 0)
            first(0, 1)
            with pe.Fori(0, B - 1) as t:
                body(t)
            body(B - 1, last=True)


def third_graph(nc, ps, res, d):
    with Stage() as ctx:
        def sb(n, s, dt=F32):
            return ctx.enter_context(nc.sbuf_tensor(f"f_{n}", s, dt))

        def sem(n):
            return ctx.semaphore(nc, f"f_{n}")

        ln = Norm(nc, ctx, "fln", ps, res.ident, res.epst)
        raw = sb("raw", [P, K, N])
        aH, aL = sb("aH", [P, K, N], F32R), sb("aL", [P, K, N], F32R)
        graw = sb("graw", [P, 2, P])
        gH, gL = sb("gH", [P, 2, P], F32R), sb("gL", [P, 2, P], F32R)
        gb = sb("gb", [P, 2, P])
        xH, xL = sb("xH", [P, 2, N], F32R), sb("xL", [P, 2, N], F32R)
        zf = [sb(f"zf{y}", [P, N]) for y in range(2)]
        zH = [sb(f"zH{y}", [P, 2, N], F32R) for y in range(2)]
        zL = [sb(f"zL{y}", [P, 2, N], F32R) for y in range(2)]
        hH, hL = sb("hH", [P, 2, N], F32R), sb("hL", [P, 2, N], F32R)
        ain, gin, lin, wh, wl, lwh, lwl, bias = (sem(n) for n in (
            "adj_in", "graph_in", "lstm_in", "w_high", "w_low", "lstm_high", "lstm_low", "bias"))
        xh, hh, hl = sem("x_high"), sem("h_high"), sem("h_low")
        za = [sem(f"z_sums{y}") for y in range(2)]
        zfd = [sem(f"z{y}") for y in range(2)]
        zh = [sem(f"z_high{y}") for y in range(2)]
        zl = [sem(f"z_low{y}") for y in range(2)]
        ab = [sem(f"a_sums{y}") for y in range(2)]
        oh, ol = sem("out_high"), sem("out_low")
        block = ctx.block(nc)
        pieces = 2 * 4 * NG * P // N

        @block.sync
        def _(sp):
            sp.dma_start(raw[:], d["adjT"]).then_inc(ain, 16)
            sp.dma_start(graw[:], d["gnw"].rearrange("p (y n) -> p y n", n=P)).then_inc(gin, 16)
            for y in range(2):
                sp.dma_start(gb[:, y, :], d["gnb"][y].partition_broadcast(P)).then_inc(gin, 16)
            for t in range(pieces):
                if t < K:
                    sp.wait_ge(wl, t + 1)
                else:
                    sp.wait_ge(lwl, t - K + 1)
                sp.dma_start(raw[:, t % K, :], d["lw"][:, t * N:(t + 1) * N]).then_inc(lin, 16)
                sp.wait_ge(lin, 16 * (t + 1))

        @block.gpsimd
        def _(pool):
            pool.sem_inc(ln.src_ready, 2)

            def take(t, u):
                ln.wait_src(pool, t)
                pool.tensor_copy(ln.src[:, u, :], res.X[:, cols(t)]).then_inc(ln.src_ready, 1)

            def weights(t):
                pool.wait_ge(lin, 16 * (t + 1))
                pool.tensor_copy(res.lwH[:, t * N:(t + 1) * N], raw[:, t % K, :]).then_inc(lwh, 1)
                pool.wait_ge(lwh, t + 1)
                pool.tensor_tensor(res.lwL[:, t * N:(t + 1) * N], raw[:, t % K, :],
                                   res.lwH[:, t * N:(t + 1) * N].bitcast(F32), ALU.subtract).then_inc(lwl, 1)

            staggered(pool, B, [(take, 0)])
            for t in range(pieces):
                weights(t)

        @block.scalar
        def _(act):
            act.sem_inc(ln.normed, 2)
            act.wait_ge(ain, 16)
            for k in range(K):
                act.activation(aH[:, k, :], raw[:, k, :], ACT.Copy).then_inc(wh, 1)
            act.wait_ge(gin, 48)
            act.activation(gH[:], graw[:], ACT.Copy).then_inc(wh, 1)

            def x_hi(t, u):
                ln.wait_out(act, t)
                act.wait_ge(za[0], t + 1)
                act.activation(xH[:, u, :], ps[2 + u][:, :], ACT.Copy).then_inc(xh, 1)

            def z_hi(y):
                def fn(t, u):
                    act.wait_ge(zfd[y], t + 2)
                    act.wait_ge(ab[y], t + 1)
                    act.activation(zH[y][:, u, :], zf[y][:, :], ACT.Copy).then_inc(zh[y], 1)
                return fn

            def h_hi(t, u):
                act.wait_ge(ab[0], t + 3)
                act.wait_ge(za[1], t + 1)
                act.activation(hH[:, u, :], ps[5][:, :], ACT.Relu).then_inc(hh, 1)

            def out_hi(t, u):
                act.wait_ge(ab[1], t + 3)
                act.activation(res.HH[:, cols(t)], ps[7][:, :], ACT.Relu).then_inc(oh, 1)

            staggered(act, B, [(x_hi, 2), (ln.deviations(act), 1), (h_hi, 3), (ln.scale(act), 1),
                               (z_hi(0), 2), (out_hi, 4), (z_hi(1), 3)])

        @block.vector
        def _(dve):
            dve.sem_inc(ln.open, 1)
            dve.sem_inc(ln.out_free, 2)
            for y in range(2):
                dve.sem_inc(zfd[y], 1)
                dve.sem_inc(zl[y], 1)
            dve.sem_inc(hl, 1)
            dve.sem_inc(ol, 1)
            for k in range(K):
                dve.wait_ge(wh, k + 1)
                dve.tensor_tensor(aL[:, k, :], raw[:, k, :], aH[:, k, :].bitcast(F32),
                                  ALU.subtract).then_inc(wl, 1)
            dve.wait_ge(wh, K + 1)
            dve.tensor_tensor(gL[:], graw[:], gH[:].bitcast(F32), ALU.subtract).then_inc(wl, 1)
            dve.tensor_tensor(res.lb[:, :], res.cols("bih"), res.cols("bhh"), ALU.add).then_inc(bias, 1)

            def x_lo(t, u):
                dve.wait_ge(xh, t + 1)
                dve.wait_ge(za[0], t + 1)
                dve.tensor_tensor(xL[:, u, :], ps[2 + u][:, :], xH[:, u, :].bitcast(F32),
                                  ALU.subtract).then_inc(ln.out_free, 1)

            def z(y):
                def fn(t, u):
                    dve.wait_ge(za[y], t + 3)
                    dve.wait_ge(zl[y], t + 1)
                    dve.tensor_tensor(zf[y][:, :].rearrange("p (k n) -> p k n", n=P),
                                      ps[4 + 2 * y][:, :].rearrange("p (k n) -> p k n", n=P),
                                      gb[:, y, :].unsqueeze(1).to_broadcast([P, K, P]),
                                      ALU.add).then_inc(zfd[y], 1)
                return fn

            def z_lo(y):
                def fn(t, u):
                    dve.wait_ge(zh[y], t + 1)
                    dve.tensor_tensor(zL[y][:, u, :], zf[y][:, :], zH[y][:, u, :].bitcast(F32),
                                      ALU.subtract).then_inc(zl[y], 1)
                return fn

            def h_lo(t, u):
                dve.wait_ge(hh, t + 1)
                dve.scalar_tensor_tensor(hL[:, u, :], ps[5][:, :], 0.0, hH[:, u, :].bitcast(F32),
                                         ALU.max, ALU.subtract).then_inc(hl, 1)

            def out_lo(t, u):
                dve.wait_ge(oh, t + 1)
                dve.scalar_tensor_tensor(res.HL[:, cols(t)], ps[7][:, :], 0.0,
                                         res.HH[:, cols(t)].bitcast(F32), ALU.max,
                                         ALU.subtract).then_inc(ol, 1)

            staggered(dve, B, [(z_lo(1), 4), (x_lo, 2), (ln.moments(dve), 1), (h_lo, 3), (z(0), 2),
                               (ln.scales(dve), 1), (z_lo(0), 2), (out_lo, 4), (z(1), 3)])

        @block.tensor
        def _(pe):
            for s in (ln.turned, ln.back, za[0], za[1], ab[0], ab[1]):
                pe.sem_inc(s, 2)
            pe.wait_ge(wl, K + 1)

            def project(y):
                def fn(t, u):
                    if y == 0:
                        pe.wait_ge(ln.out_free, t + 3)
                    else:
                        pe.wait_ge(hl, t + 2)
                    pe.wait_ge(zfd[y], t + 1)
                    for k in range(K):
                        h, lo = ((xH, xL), (hH, hL))[y]
                        ins = three(pe, ps[4 + 2 * y][:, k * P:(k + 1) * P], h[:, u, k * P:(k + 1) * P],
                                    lo[:, u, k * P:(k + 1) * P], gH[:, y, :], gL[:, y, :], True, True)
                    ins.then_inc(za[y], 1)
                return fn

            def aggregate(y):
                def fn(t, u):
                    pe.wait_ge(zl[y], t + 2)
                    pe.wait_ge((hl, ol)[y], t + 1)
                    for k in range(K):
                        w = slice(k * P, (k + 1) * P)
                        ins = three(pe, ps[5 + 2 * y][:, :], zH[y][:, u, w], zL[y][:, u, w], aH[:, k, :],
                                    aL[:, k, :], k == 0, k == K - 1)
                    ins.then_inc(ab[y], 1)
                return fn

            staggered(pe, B, [(aggregate(0), 3), (project(0), 2), (aggregate(1), 4), (project(1), 3),
                              (ln.turn(pe), 0), (ln.turn_back(pe), 1)])


class Windows:

    def __init__(self, p, nb, groups, before, recur_before):
        self.p, self.nb, self.groups = p, nb, groups
        self.nw = S // p
        self.n = nb * self.nw
        self.chains = B // nb // groups
        self.units = [(s, c) for s in range(p) for c in range(self.chains)]
        self.before = before
        self.recur_before = recur_before
        self.after = before + groups * len(self.units)
        self.recur = groups * (p - 1) * self.chains

    def count(self, g, i):
        return g * len(self.units) + (self.before + i)

    def recurrent(self, g, i):
        return g * ((self.p - 1) * self.chains) + (self.recur_before + max(0, i - self.chains))

    def tokens(self, a, g, c, s):
        w = self.nb * S
        v = a[:, bass.ds(g * (self.chains * w) + c * w, w)]
        v = v.rearrange("q (b m) -> q b m", m=S)
        return v[:, :, s:s + self.p * (self.nw - 1) + 1:self.p]

    def shaped(self, a):
        return a.rearrange("q (b m) -> q b m", m=self.nw)


def lstms(nc, ps, res):
    with Stage() as ctx:
        def sb(n, s, dt=F32):
            return ctx.enter_context(nc.sbuf_tensor(f"g_{n}", s, dt))

        def sem(n):
            return ctx.semaphore(nc, f"g_{n}")

        gates = sb("gates", [P, 2, NG, N])
        TC, IG, hf = sb("TC", [P, 2, N]), sb("IG", [P, 2, N]), sb("hf", [P, 2, N])
        C = sb("C", [P, 4, N])
        sH, sL = sb("sH", [P, 4, N], F32R), sb("sL", [P, 4, N], F32R)
        C1st = sb("C1", [P, 2, N])
        sums, gated, igd, fcd, cell, tcd, hfd, hhd, outd = (sem(n) for n in (
            "sums", "gated", "ig", "fc", "cell", "tanh_cell", "h", "h_high", "h_low"))
        block = ctx.block(nc)
        plan = []
        for p, nb, groups in ((1, 1, 2), (2, 2, 2), (3, 2, 2), (4, 4, 1)):
            last = plan[-1] if plan else None
            plan.append(Windows(p, nb, groups, last.after if last else 0,
                                last.recur_before + last.recur if last else 0))

        def run(eng, emit):
            for w in plan:
                if w.groups == 1:
                    emit(w, 0)
                else:
                    with eng.Fori(0, w.groups) as g:
                        emit(w, g)

        def cells(w, i):
            s, c = w.units[i]
            if w.p == 1:
                return C1st[:, i % 2, 0:w.n]
            return C[:, c, 0:w.n]

        @block.tensor
        def _(pe):
            def emit(w, g):
                for i, (s, c) in enumerate(w.units):
                    k = w.count(g, i)
                    u = i % 2
                    pe.wait_ge(gated, k + 1)
                    if s:
                        pe.wait_ge(outd, k - w.chains + 3)
                    elif w.p == 2:
                        pe.wait_ge(outd, g * (2 * w.chains) + (2 * c + 4))
                    elif w.p == 3:
                        pe.wait_ge(outd, g * 8 + (plan[1].before + w.chains + c + 3))
                    elif w.p == 4:
                        o = 2 * c + 1
                        pe.wait_ge(outd, plan[2].before + 12 * (o // 4) + 8 + o % 4 + 3)
                    xh, xl = w.tokens(res.HH, g, c, s), w.tokens(res.HL, g, c, s)
                    hh, hl = w.shaped(sH[:, c % 4, 0:w.n]), w.shaped(sL[:, c % 4, 0:w.n])
                    for gate in (0, 1, 2, 3):
                        if gate == 1 and not s:
                            continue
                        bank = w.shaped(ps[4 * u + gate][:, 0:w.n])
                        o = ((w.p - 1) * NG + gate) * P
                        ins = three(pe, bank, res.lwH[:, o:o + P], res.lwL[:, o:o + P], xh, xl,
                                    True, not s)
                        if s:
                            o += 4 * NG * P
                            ins = three(pe, bank, res.lwH[:, o:o + P], res.lwL[:, o:o + P], hh, hl,
                                        False, True)
                    ins.then_inc(sums, 1)

            pe.sem_inc(sums, 1)
            run(pe, emit)

        @block.scalar
        def _(act):
            act.sem_inc(gated, 2)

            def tanh_cell(w, g, i):
                k, u = w.count(g, i), i % 2
                act.wait_ge(cell, k + 1)
                act.activation(TC[:, u, 0:w.n], cells(w, i), ACT.Tanh).then_inc(tcd, 1)

            def emit(w, g):
                for i, (s, c) in enumerate(w.units):
                    k, u = w.count(g, i), i % 2
                    act.wait_ge(sums, k + 2)
                    act.wait_ge(outd, k + 1)
                    for gate in ((0, 2, 3) if not s else (0, 2, 1, 3)):
                        o = (w.p - 1) * NG + gate
                        ins = act.activation(gates[:, u, gate, 0:w.n], ps[4 * u + gate][:, 0:w.n],
                                             ACT.Tanh if gate == 2 else ACT.Sigmoid,
                                             bias=res.lb[:, o:o + 1])
                    ins.then_inc(gated, 1)
                    if i:
                        tanh_cell(w, g, i - 1)
                tanh_cell(w, g, len(w.units) - 1)

            run(act, emit)

        @block.vector
        def _(dve):
            dve.sem_inc(outd, 2)

            def update(w, g, i):
                s, c = w.units[i]
                k, u, n = w.count(g, i), i % 2, w.n
                dve.wait_ge(gated, k + 3)
                if not s:
                    dve.tensor_tensor(cells(w, i), gates[:, u, 0, 0:n], gates[:, u, 2, 0:n],
                                      ALU.mult).then_inc(cell, 1)
                    return
                r = w.recurrent(g, i)
                dve.tensor_tensor(IG[:, u, 0:n], gates[:, u, 0, 0:n], gates[:, u, 2, 0:n],
                                  ALU.mult).then_inc(igd, 1)
                dve.tensor_tensor(C[:, c, 0:n], gates[:, u, 1, 0:n], C[:, c, 0:n],
                                  ALU.mult).then_inc(fcd, 1)
                dve.wait_ge(igd, r + 1)
                dve.wait_ge(fcd, r + 1)
                dve.tensor_tensor(C[:, c, 0:n], IG[:, u, 0:n], C[:, c, 0:n], ALU.add).then_inc(cell, 1)

            def output(w, g, i):
                s, c = w.units[i]
                k, u, n = w.count(g, i), i % 2, w.n
                dve.wait_ge(tcd, k + 1)
                dve.tensor_tensor(hf[:, u, 0:n], gates[:, u, 3, 0:n], TC[:, u, 0:n],
                                  ALU.mult).then_inc(hfd, 1)
                if s < w.p - 1:
                    hi, lo = w.shaped(sH[:, c, 0:n]), w.shaped(sL[:, c, 0:n])
                else:
                    hi, lo = w.tokens(res.HH, g, c, s), w.tokens(res.HL, g, c, s)
                dve.wait_ge(hfd, k + 1)
                dve.tensor_copy(hi, w.shaped(hf[:, u, 0:n])).then_inc(hhd, 1)
                dve.wait_ge(hhd, k + 1)
                dve.tensor_tensor(lo, w.shaped(hf[:, u, 0:n]), hi.bitcast(F32),
                                  ALU.subtract).then_inc(outd, 1)

            def emit(w, g):
                for i in range(len(w.units)):
                    update(w, g, i)
                    if i:
                        output(w, g, i - 1)
                output(w, g, len(w.units) - 1)

            run(dve, emit)


def routing(nc, ps, res, XN, d, rt):
    with Stage() as ctx:
        def sb(n, s, dt=F32):
            return ctx.enter_context(nc.sbuf_tensor(f"h_{n}", s, dt))

        def sem(n):
            return ctx.semaphore(nc, f"h_{n}")

        ln = Norm(nc, ctx, "hln", ps, res.ident, res.epst)
        hs = sb("hs", [P, 2, N])
        xsum = sb("xsum", [P, B])
        wr, br = sb("wr", [P, E]), sb("br", [B, E])
        b2 = sb("b2", [E, P])
        rank, ones = sb("rank", [B, E]), sb("ones", [B, P])
        names = ("logit", "ex", "rw", "ratio", "over", "scale", "z", "ex2", "w2", "eq", "o1", "o2", "masked",
                 "dense", "idx")
        a = {n: sb(n, [B, E]) for n in names}
        col = {n: sb(n, [B, 1]) for n in ("m", "nm", "den", "rden", "m1", "m2", "x1", "x2", "e2", "p1", "p2",
                                          "i1", "i2", "dd")}
        pd = sb("pd", [B, 2, B])
        row = sb("row", [1, 2 * B])
        denseT = sb("denseT", [E, B])
        hsum, copied, win, rk, xs = (sem(n) for n in ("hsum", "copied", "in", "rank", "x_sums"))
        step, acts, mm, ev = (sem(n) for n in ("step", "acts", "mm", "ev"))
        block = ctx.block(nc)

        @block.sync
        def _(sp):
            sp.dma_start(wr[:], d["wr"]).then_inc(win, 16)
            sp.dma_start(br[:], d["br"][0].partition_broadcast(B)).then_inc(win, 16)
            sp.dma_start(b2[:], d["hb2"]).then_inc(win, 16)
            sp.wait_ge(win, 48)

        @block.gpsimd
        def _(pool):
            for e in range(E):
                pool.memset(rank[:, e:e + 1], float(E - e)).then_inc(rk, 1)
            pool.memset(ones[:, :], 1.0).then_inc(rk, 1)
            pool.sem_inc(copied, 2)

            def keep_x(t, u):
                pool.wait_ge(ln.src_ready, t + 3)
                pool.tensor_copy(res.X[:, cols(t)], ln.src[:, u, :]).then_inc(copied, 1)

            staggered(pool, B, [(keep_x, 0)])

        @block.scalar
        def _(act):
            act.sem_inc(ln.normed, 2)
            act.sem_inc(ln.out_free, 2)

            def evac(t, u):
                ln.wait_out(act, t)
                act.activation(XN[:, cols(t)], ps[2 + u][:, :], ACT.Copy,
                               accum_out=xsum[:, bass.ds(t, 1)]).then_inc(ln.out_free, 1)

            staggered(act, B, [(ln.deviations(act), 1), (evac, 2), (ln.scale(act), 1)])
            act.wait_ge(step, 3)
            act.activation(a["ex"][:, :], a["logit"][:, :], ACT.Exp, bias=col["nm"][:, 0:1]).then_inc(acts, 1)
            act.wait_ge(step, 14)
            act.activation(a["ex2"][:, :], a["z"][:, :], ACT.Exp, bias=col["nm"][:, 0:1]).then_inc(acts, 1)
            act.wait_ge(step, 27)
            act.activation(col["e2"][:, :], col["dd"][:, :], ACT.Exp).then_inc(acts, 1)

        @block.vector
        def _(dve):
            dve.sem_inc(ln.open, 1)
            dve.sem_inc(ln.src_ready, 2)

            def add(t, u):
                dve.tensor_tensor(hs[:, u, :], res.HH[:, cols(t)].bitcast(F32),
                                  res.HL[:, cols(t)].bitcast(F32), ALU.add).then_inc(hsum, 1)
                dve.wait_ge(hsum, t + 1)
                ln.wait_src(dve, t)
                dve.wait_ge(copied, t + 1)
                dve.tensor_tensor(ln.src[:, u, :], hs[:, u, :], res.X[:, cols(t)],
                                  ALU.add).then_inc(ln.src_ready, 1)

            staggered(dve, B, [(add, 0), (ln.moments(dve), 1), (ln.scales(dve), 1)])

            done = [0]

            def then(ins):
                ins.then_inc(step, 1)
                done[0] += 1
                dve.wait_ge(step, done[0])

            def wide(v):
                return v[:, 0:1].to_broadcast([B, E])

            def tt(o, x, y, op):
                then(dve.tensor_tensor(o, x, y, op))

            dve.wait_ge(win, 48)
            dve.wait_ge(rk, E + 1)
            dve.wait_ge(mm, 1)
            then(dve.scalar_tensor_tensor(a["logit"][:], ps[0][0:B, 0:E], 1.0 / S, br[:, :], ALU.mult, ALU.add))
            then(dve.tensor_reduce(col["m"][:], a["logit"][:], AX.X, ALU.max))
            then(dve.tensor_scalar(col["nm"][:], col["m"][:], -1.0, None, ALU.mult))
            dve.wait_ge(acts, 1)
            then(dve.tensor_reduce(col["den"][:], a["ex"][:], AX.X, ALU.add))
            then(dve.reciprocal(col["rden"][:], col["den"][:]))
            tt(a["rw"][:], a["ex"][:], wide(col["rden"]), ALU.mult)
            dve.wait_ge(mm, 2)
            then(dve.tensor_scalar(a["scale"][:], ps[1][0:B, 0:E], float(S), None, ALU.mult))
            then(dve.reciprocal(a["ratio"][:], a["scale"][:]))
            then(dve.tensor_scalar(a["over"][:], a["scale"][:], CAP, None, ALU.is_gt))
            then(dve.tensor_scalar(a["ratio"][:], a["ratio"][:], CAP, -1.0, ALU.mult, ALU.add))
            tt(a["ratio"][:], a["ratio"][:], a["over"][:], ALU.mult)
            then(dve.scalar_tensor_tensor(a["z"][:], a["ratio"][:], 1.0, a["rw"][:], ALU.add, ALU.mult))
            then(dve.tensor_reduce(col["m"][:], a["z"][:], AX.X, ALU.max))
            then(dve.tensor_scalar(col["nm"][:], col["m"][:], -1.0, None, ALU.mult))
            dve.wait_ge(acts, 2)
            then(dve.tensor_reduce(col["den"][:], a["ex2"][:], AX.X, ALU.add))
            then(dve.reciprocal(col["rden"][:], col["den"][:]))
            tt(a["w2"][:], a["ex2"][:], wide(col["rden"]), ALU.mult)
            then(dve.tensor_reduce(col["m1"][:], a["w2"][:], AX.X, ALU.max))
            tt(a["eq"][:], a["w2"][:], wide(col["m1"]), ALU.is_equal)
            tt(a["eq"][:], a["eq"][:], rank[:, :], ALU.mult)
            then(dve.tensor_reduce(col["x1"][:], a["eq"][:], AX.X, ALU.max))
            tt(a["o1"][:], a["eq"][:], wide(col["x1"]), ALU.is_equal)
            then(dve.scalar_tensor_tensor(a["masked"][:], a["o1"][:], -BIG, a["w2"][:], ALU.mult, ALU.add))
            then(dve.tensor_reduce(col["m2"][:], a["masked"][:], AX.X, ALU.max))
            tt(a["eq"][:], a["masked"][:], wide(col["m2"]), ALU.is_equal)
            tt(a["eq"][:], a["eq"][:], rank[:, :], ALU.mult)
            tt(col["dd"][:], col["m2"][:], col["m1"][:], ALU.subtract)
            then(dve.tensor_reduce(col["x2"][:], a["eq"][:], AX.X, ALU.max))
            tt(a["o2"][:], a["eq"][:], wide(col["x2"]), ALU.is_equal)
            dve.wait_ge(acts, 3)
            then(dve.tensor_scalar(col["den"][:], col["e2"][:], 1.0, None, ALU.add))
            then(dve.reciprocal(col["p1"][:], col["den"][:]))
            tt(col["p2"][:], col["e2"][:], col["p1"][:], ALU.mult)
            tt(a["o1"][:], a["o1"][:], wide(col["p1"]), ALU.mult)
            tt(a["o2"][:], a["o2"][:], wide(col["p2"]), ALU.mult)
            tt(a["dense"][:], a["o1"][:], a["o2"][:], ALU.add)
            then(dve.tensor_scalar(col["i1"][:], col["x1"][:], -1.0, float(E), ALU.mult, ALU.add))
            then(dve.tensor_scalar(col["i2"][:], col["x2"][:], -1.0, float(E), ALU.mult, ALU.add))
            then(dve.tensor_scalar(pd[:, 0, :], res.ident[0:B, 0:B], col["p1"][:, 0:1], None, ALU.mult))
            then(dve.tensor_scalar(pd[:, 1, :], res.ident[0:B, 0:B], col["p2"][:, 0:1], None, ALU.mult))
            dve.wait_ge(mm, 3)
            then(dve.tensor_copy(rt.index[:, :], ps[2][0:1, 0:2 * B]))
            then(dve.tensor_copy(rt.weight[:].rearrange("p x b -> p (x b)"), ps[3][:, 0:2 * B]))
            then(dve.tensor_copy(denseT[:, :], ps[4][0:E, 0:B]))
            dve.wait_ge(mm, 4)
            then(dve.tensor_copy(rt.bias2[:, :], ps[5][:, 0:B]))

        @block.tensor
        def _(pe):
            pe.sem_inc(ln.turned, 2)
            pe.sem_inc(ln.back, 2)
            staggered(pe, B, [(ln.turn(pe), 0), (ln.turn_back(pe), 1)])
            pe.wait_ge(win, 48)
            pe.wait_ge(ln.out_free, B + 2)
            pe.matmul(ps[0][0:B, 0:E], xsum[:, :], wr[:, :], start=True, stop=True).then_inc(mm, 1)
            pe.wait_ge(rk, E + 1)
            pe.wait_ge(step, 6)
            pe.matmul(ps[1][0:B, 0:E], ones[:, 0:B], a["rw"][:, :], start=True, stop=True).then_inc(mm, 1)
            pe.wait_ge(step, 39)
            for x, c in enumerate(("i1", "i2")):
                pe.matmul(ps[2][0:1, x * B:(x + 1) * B], col[c][:, 0:1], res.ident[0:B, 0:B],
                          start=True, stop=True)
            pe.matmul(ps[3][:, 0:2 * B], ones[:, :], pd[:].rearrange("p x b -> p (x b)"), start=True, stop=True)
            pe.transpose(ps[4][0:E, 0:B], a["dense"][:, :], res.ident[0:B, 0:B]).then_inc(mm, 1)
            pe.wait_ge(step, 42)
            pe.matmul(ps[5][:, 0:B], b2[:, :], denseT[:, :], start=True, stop=True).then_inc(mm, 1)


def chosen_experts(nc, ps, res, XN, d, rt):
    F = 2 * GJ
    with Stage() as ctx:
        def sb(n, s, dt=F32):
            return ctx.enter_context(nc.sbuf_tensor(f"i_{n}", s, dt))

        def sem(n):
            return ctx.semaphore(nc, f"i_{n}")

        raw = sb("raw", [P, 2, 2, EW])
        b1 = sb("b1", [P, 2, 2, GJ])
        wH, wL = sb("wH", [P, 2, 2, EW], F32R), sb("wL", [P, 2, 2, EW], F32R)
        xH, xL = sb("xH", [P, 2, N], F32R), sb("xL", [P, 2, N], F32R)
        hf = sb("hf", [P, F, N])
        hH, hL = sb("hH", [P, F, N], F32R), sb("hL", [P, F, N], F32R)
        win = [sem("weights_even"), sem("weights_odd")]
        scaled, wh, wl, xh, xl = (sem(n) for n in ("scaled", "w_high", "w_low", "x_high", "x_low"))
        m1, m2, hfd, hhd, lod, outd = (sem(n) for n in ("hidden_sums", "hidden_used", "hidden", "h_high",
                                                        "h_low", "out"))
        block = ctx.block(nc)

        @block.sync
        def _(sp):
            def load(t, u, n):
                for x in range(2):
                    e = sp.value_load(rt.index[0:1, bass.ds(x * B + t, 1)], min_val=0, max_val=E - 1)
                    sp.dma_start(raw[:, u, x, :], d["hw"][bass.ds(e, 1)].rearrange("o p n -> (o p) n"))\
                        .then_inc(win[u], 16)
                    sp.dma_start(b1[:, u, x, :], d["hb1"][bass.ds(e, 1)].rearrange("o p n -> (o p) n"))\
                        .then_inc(win[u], 16)

            for t in range(B):
                if t >= 2:
                    sp.wait_ge(wl, t - 1)
                    sp.wait_ge(hhd, (t - 1) * F)
                load(t, t % 2, t // 2)

        @block.gpsimd
        def _(pool):
            def low(t, u):
                pool.wait_ge(wh, t + 1)
                pool.tensor_tensor(wL[:, u], raw[:, u], wH[:, u].bitcast(F32), ALU.subtract).then_inc(wl, 1)

            staggered(pool, B, [(low, 0)])

        @block.scalar
        def _(act):
            def hidden(t, u):
                for q in range(F):
                    x, f = q // GJ, q % GJ
                    act.wait_ge(m1, t * F + (q + 1))
                    act.wait_ge(lod, t * F + (q + 1))
                    act.activation(hf[:, q, :], ps[q][:, :], ACT.Gelu, bias=b1[:, u, x, f:f + 1])\
                        .then_inc(hfd, 1)
                    act.wait_ge(m2, t * F + (q + 1))
                    act.activation(hH[:, q, :], ps[q][:, :], ACT.Gelu, bias=b1[:, u, x, f:f + 1])\
                        .then_inc(hhd, 1)

            staggered(act, B, [(hidden, 0)])

        @block.vector
        def _(dve):
            dve.sem_inc(lod, F)
            dve.sem_inc(outd, 2)

            def weights(t, u):
                if isinstance(t, int):
                    dve.wait_ge(win[u], 64 * (t // 2 + 1))
                else:
                    dve.wait_ge(win[u], t * 32 + (64 - 32 * u))
                for x in range(2):
                    w2 = raw[:, u, x, GH:EW]
                    ins = dve.tensor_scalar(w2, w2, rt.weight[:, x, bass.ds(t, 1)], None, ALU.mult)
                ins.then_inc(scaled, 1)
                dve.wait_ge(scaled, t + 1)
                dve.wait_ge(outd, t + 1)
                dve.tensor_copy(wH[:, u], raw[:, u]).then_inc(wh, 1)

            def x_parts(t, u):
                dve.wait_ge(outd, t + 1)
                dve.tensor_copy(xH[:, u, :], XN[:, cols(t)]).then_inc(xh, 1)
                dve.wait_ge(xh, t + 1)
                dve.tensor_tensor(xL[:, u, :], XN[:, cols(t)], xH[:, u, :].bitcast(F32),
                                  ALU.subtract).then_inc(xl, 1)

            def low(t, u):
                for q in range(F):
                    dve.wait_ge(hfd, t * F + (q + 1))
                    dve.wait_ge(hhd, t * F + (q + 1))
                    dve.wait_ge(m2, t * F + (q + 1))
                    dve.tensor_tensor(hL[:, q, :], hf[:, q, :], hH[:, q, :].bitcast(F32),
                                      ALU.subtract).then_inc(lod, 1)

            def add(t, u):
                dve.wait_ge(m2, t * F + 2 * F)
                dve.scalar_tensor_tensor(XN[:, cols(t)], ps[4 + u][:, :], rt.bias2[:, bass.ds(t, 1)],
                                         XN[:, cols(t)], ALU.add, ALU.add).then_inc(outd, 1)

            staggered(dve, B, [(add, 2), (weights, 0), (x_parts, 0), (low, 1)])

        @block.tensor
        def _(pe):
            pe.sem_inc(m2, F)

            def first(t, u):
                pe.wait_ge(wl, t + 1)
                pe.wait_ge(xl, t + 1)
                for q in range(F):
                    x, f = q // GJ, q % GJ
                    pe.wait_ge(lod, t * F + (q + 1))
                    w = slice(f * P, (f + 1) * P)
                    three(pe, ps[q][:, :], wH[:, u, x, w], wL[:, u, x, w], xH[:, u, :], xL[:, u, :],
                          True, True).then_inc(m1, 1)

            def second(t, u):
                for q in range(F):
                    x, f = q // GJ, q % GJ
                    pe.wait_ge(lod, t * F + (q + 1 + F))
                    w = slice(GH + f * P, GH + (f + 1) * P)
                    three(pe, ps[4 + u][:, :], wH[:, u, x, w], wL[:, u, x, w], hH[:, q, :], hL[:, q, :],
                          q == 0, q == F - 1).then_inc(m2, 1)

            staggered(pe, B, [(first, 0), (second, 1)])


def final_norm(nc, ps, res, XN, out):
    with Stage() as ctx:
        def sb(n, s, dt=F32):
            return ctx.enter_context(nc.sbuf_tensor(f"j_{n}", s, dt))

        def sem(n):
            return ctx.semaphore(nc, f"j_{n}")

        ln = Norm(nc, ctx, "jln", ps, res.ident, res.epst)
        z, o = sb("z", [P, 2, N]), sb("o", [P, 2, N])
        addd, stored = sem("added"), sem("stored")
        block = ctx.block(nc)

        @block.sync
        def _(sp):
            sp.sem_inc(stored, 32)
            for t in range(B):
                sp.wait_ge(addd, t + 3)
                sp.wait_ge(stored, 16 * (t + 2))
                sp.dma_start(out[:, t * N:(t + 1) * N], o[:, t % 2, :]).then_inc(stored, 16)
            sp.wait_ge(stored, 16 * (B + 2))

        @block.gpsimd
        def _(pool):
            pool.sem_inc(ln.src_ready, 2)

            def take(t, u):
                ln.wait_src(pool, t)
                pool.tensor_copy(ln.src[:, u, :], XN[:, cols(t)]).then_inc(ln.src_ready, 1)

            staggered(pool, B, [(take, 0)])

        @block.scalar
        def _(act):
            act.sem_inc(ln.normed, 2)
            act.sem_inc(ln.out_free, 2)

            def affine(t, u):
                ln.wait_out(act, t)
                act.wait_ge(addd, t + 1)
                act.activation(z[:, u, :], ps[2 + u][:, :], ACT.Identity, bias=res.col("beta", 0),
                               scale=res.col("gamma", 0)).then_inc(ln.out_free, 1)

            staggered(act, B, [(ln.deviations(act), 1), (affine, 2), (ln.scale(act), 1)])

        @block.vector
        def _(dve):
            dve.sem_inc(ln.open, 1)
            dve.sem_inc(addd, 2)

            def add(t, u):
                dve.wait_ge(ln.out_free, t + 3)
                dve.wait_ge(stored, t * 16 + 16)
                dve.tensor_tensor(o[:, u, :], z[:, u, :], res.X[:, cols(t)], ALU.add).then_inc(addd, 1)

            staggered(dve, B, [(ln.moments(dve), 1), (add, 2), (ln.scales(dve), 1)])

        @block.tensor
        def _(pe):
            pe.sem_inc(ln.turned, 2)
            pe.sem_inc(ln.back, 2)
            staggered(pe, B, [(ln.turn(pe), 0), (ln.turn_back(pe), 1)])


class Resident:

    def col(self, name, i):
        a = VEC[name][0] + i
        return self.vec[:, a:a + 1]

    def cols(self, name):
        a, b = VEC[name]
        return self.vec[:, a:b]


def build(nc, d, out):
    with ExitStack() as ctx:
        def keep(c, name, shape, dt=F32):
            return c.enter_context(nc.sbuf_tensor(name, shape, dt))

        ps = [ctx.enter_context(nc.psum_tensor(f"bank{i}", [P, N], F32)) for i in range(8)]
        res = Resident()
        res.X = keep(ctx, "X", [P, TOK])
        res.vec = keep(ctx, "vec", [P, NVEC])
        res.ident = keep(ctx, "ident", [P, P])
        res.epst = keep(ctx, "epst", [P, 1])
        with ExitStack() as first:
            Y2 = keep(first, "Y2", [P, TOK])
            res.xt = Y2[:].rearrange("p (t n) -> p t n", n=P)
            res.st2 = keep(first, "st2", [P, 1, B, 6])
            with ExitStack() as graph:
                res.gwH = keep(graph, "gwH", [P, H1 + C1 * P], F32R)
                res.gwL = keep(graph, "gwL", [P, H1 + C1 * P], F32R)
                res.st1 = keep(graph, "st1", [P, C1, B, 6])
                res.ahH = keep(graph, "ahH", [P, K, N], F32R)
                res.ahL = keep(graph, "ahL", [P, K, N], F32R)
                res.rs0 = keep(graph, "rs0", [P, B * K])
                res.nmr0 = keep(graph, "nmr0", [P, B * K])
                prepare(nc, ps, d, res)
                Y1 = keep(graph, "Y1", [P, C1, TOK])
                first_graph(nc, ps, res, Y1)
                second_graph(nc, ps, res, Y1, Y2)
            fwH = keep(first, "fwH", [P, 2 * E * FH], F32R)
            fwL = keep(first, "fwL", [P, 2 * E * FH], F32R)
            combine = nc.dram_tensor("combine", [K, P, P], F32, kind="Internal").ap()
            gate_stage(nc, ps, res, Y2, fwH, fwL, d, combine)
            experts(nc, ps, res, Y2, fwH, fwL, combine)
        res.HH = keep(ctx, "HH", [P, TOK], F32R)
        res.HL = keep(ctx, "HL", [P, TOK], F32R)
        with ExitStack() as recurrent:
            res.lwH = keep(recurrent, "lwH", [P, 2 * 4 * NG * P], F32R)
            res.lwL = keep(recurrent, "lwL", [P, 2 * 4 * NG * P], F32R)
            res.lb = keep(recurrent, "lb", [P, 4 * NG])
            third_graph(nc, ps, res, d)
            lstms(nc, ps, res)
        XN = keep(ctx, "XN", [P, TOK])
        rt = Resident()
        rt.index = keep(ctx, "index", [1, 2 * B], I32)
        rt.weight = keep(ctx, "weight", [P, 2, B])
        rt.bias2 = keep(ctx, "bias2", [P, B])
        routing(nc, ps, res, XN, d, rt)
        chosen_experts(nc, ps, res, XN, d, rt)
        final_norm(nc, ps, res, XN, out)


def _layouts(i):
    import numpy as np
    c = np.ascontiguousarray
    x = i["x"]
    a = {
        "x_tm": c(x.reshape(B * K, P, D).transpose(1, 0, 2)),
        "x_fm": c(x.reshape(TOK, D).T),
        "adj": c(i["adj"].reshape(K, P, S).transpose(1, 0, 2)),
        "adjT": c(i["adj"].T.reshape(K, P, S).transpose(1, 0, 2)),
        "gw": c(np.concatenate([i["L0_gnn_W1"].T,
                                i["L0_gnn_W2"].T.reshape(C1, P, P).transpose(1, 0, 2).reshape(P, C1 * P)], 1)),
        "fw": c(np.concatenate([i["L0_ffn_W1"].transpose(2, 0, 1).reshape(P, E * FH),
                                i["L0_ffn_W2"].transpose(2, 0, 1).reshape(FJ, P, E, P).transpose(1, 2, 0, 3)
                                .reshape(P, E * FH)], 1)),
        "wg": c(i["L0_ffn_Wg"].T),
        "bg": c(i["L0_ffn_bg"].reshape(1, E)),
        "gnw": c(np.concatenate([i["L1_gnn_Wg0"], i["L1_gnn_Wg1"]], 1)),
        "gnb": c(np.stack([i["L1_gnn_bg0"], i["L1_gnn_bg1"]])),
        "lw": c(np.concatenate([i["L1_gnn_Wih"].transpose(2, 0, 1).reshape(P, 4 * NG * P),
                                i["L1_gnn_Whh"].transpose(2, 0, 1).reshape(P, 4 * NG * P)], 1)),
        "wr": c(i["L1_ffn_Wr"]),
        "br": c(i["L1_ffn_br"].reshape(1, E)),
        "hw": c(np.concatenate([i["L1_ffn_W1"].reshape(E, P, GH),
                                i["L1_ffn_W2"].reshape(E, GJ, P, P).transpose(0, 2, 1, 3).reshape(E, P, GH)], 2)),
        "hb1": c(i["L1_ffn_b1"].reshape(E, GJ, P).transpose(0, 2, 1)),
        "hb2": c(i["L1_ffn_b2"]),
    }
    vec = {
        "gb1": i["L0_gnn_b1"].reshape(C1, P).T, "gg1": i["L0_gnn_g1"].reshape(C1, P).T,
        "gbe1": i["L0_gnn_be1"].reshape(C1, P).T, "gb2": i["L0_gnn_b2"][:, None],
        "gg2": i["L0_gnn_g2"][:, None], "gbe2": i["L0_gnn_be2"][:, None],
        "fb1": i["L0_ffn_b1"].reshape(E * FJ, P).T, "fb2": i["L0_ffn_b2"].T,
        "bih": i["L1_gnn_bih"].reshape(4 * NG, P).T, "bhh": i["L1_gnn_bhh"].reshape(4 * NG, P).T,
        "hb1": i["L1_ffn_b1"].reshape(E * GJ, P).T,
        "gamma": i["L1_ffn_gamma"][:, None], "beta": i["L1_ffn_beta"][:, None],
    }
    a["vec"] = c(np.concatenate([vec[n] for n in VEC], 1))
    return a


def kernel(**inputs):
    import numpy as _np
    import concourse.bacc as _bacc
    from concourse import mybir as _mybir
    from concourse.bass_utils import run_bass_kernel_spmd as _run

    nc = _bacc.Bacc("TRN2", target_bir_lowering=False, num_devices=1)
    arrays, args = {}, {}
    for name, a in _layouts({k: _np.asarray(v) for k, v in inputs.items()}).items():
        arrays[f"in_{name}"] = a
        args[name] = nc.dram_tensor(f"in_{name}", a.shape, _mybir.dt.from_np(a.dtype), kind="ExternalInput").ap()
    out = nc.dram_tensor("out_x", (P, TOK), _mybir.dt.float32, kind="ExternalOutput").ap()
    build(nc, args, out)
    r = _run(nc, [arrays], core_ids=[0])
    return _np.ascontiguousarray(r.results[0]["out_x"].T).reshape(B, S, D)
```

```python
from contextlib import ExitStack

import concourse.bass as bass
from concourse import mybir

F32 = mybir.dt.float32
F32R = mybir.dt.float32r
I32 = mybir.dt.int32
ALU = mybir.AluOpType
ACT = mybir.ActivationFunctionType
AX = mybir.AxisListType

P = 128
B, S, D = 16, 512, 128
T = B
N = S
K = S // P
TOK = B * S
H1 = 256
C1 = H1 // P
E = 8
FH = 512
FJ = FH // P
GH = 256
GJ = GH // P
EW = 2 * GH
EPS = 1e-5
BIG = 3.0e38
NG = 4
CAP = float(-(-(TOK * 5) // (4 * E)))

VEC = {}
_at = 0
for _name, _n in (("gb1", C1), ("gg1", C1), ("gbe1", C1), ("gb2", 1), ("gg2", 1), ("gbe2", 1),
                  ("fb1", E * FJ), ("fb2", E), ("bih", 4 * NG), ("bhh", 4 * NG),
                  ("gamma", 1), ("beta", 1)):
    VEC[_name] = (_at, _at + _n)
    _at += _n
NVEC = _at


def staggered(eng, n, parts, ring=2):
    edge = max(1, -(-max(lag for _, lag in parts) // ring)) * ring
    for t in range(edge):
        for fn, lag in parts:
            if t >= lag:
                fn(t - lag, (t - lag) % ring)
    with eng.Fori(edge // ring, n // ring) as i:
        for u in range(ring):
            for fn, lag in parts:
                fn(i * ring + (u - lag), (u - lag) % ring)
    for t in range(n, n + max(lag for _, lag in parts)):
        for fn, lag in parts:
            if t - lag < n:
                fn(t - lag, (t - lag) % ring)


def cols(t, n=N, off=0):
    return bass.ds(t * n + off, n)



class Stage(ExitStack):

    def __init__(self):
        super().__init__()
        self.used = []

    def semaphore(self, nc, name):
        self.used.append(self.enter_context(nc.semaphore(name)))
        return self.used[-1]

    def block(self, nc):
        self.callback(self.clear, nc)
        return self.enter_context(nc.Block())

    def clear(self, nc):
        numbers = sorted(s.num for s in self.used)
        with nc.Block() as block:
            @block.gpsimd
            def _(pool):
                first = last = numbers[0]
                for n in numbers[1:] + [None]:
                    if n != last + 1:
                        pool.sem_clear(range(first, last + 1))
                        first = n
                    last = n


class Norm:

    def __init__(self, nc, ctx, name, ps, ident, epst, ring=2):
        self.nc, self.ps, self.ident, self.epst = nc, ps, ident, epst
        self.ring = ring
        self.bank = [ps[b] for b in (0, 1, 6, 7)[:ring]]

        def sb(n, s):
            return ctx.enter_context(nc.sbuf_tensor(f"{name}_{n}", s, F32))

        def sem(n):
            return ctx.semaphore(nc, f"{name}_{n}")

        self.src = sb("src", [P, 2, N])
        self.stats = sb("stats", [P, ring, K, 6])
        self.mv = sb("mv", [P, ring, K, 2])
        self.sd = sb("sd", [P, ring, K])
        self.rs = sb("rs", [P, ring, K])
        self.nmr = sb("nmr", [P, ring, K])
        self.gate = sb("gate", [P, 1])
        self.xt = sb("xt", [P, 2, K, P])
        self.src_ready = sem("src_ready")
        self.turned = sem("turned")
        self.stats_done = sem("stats_done")
        self.mv_done = sem("mv_done")
        self.sd_done = sem("sd_done")
        self.rs_done = sem("rs_done")
        self.nmr_done = sem("nmr_done")
        self.normed = sem("normed")
        self.back = sem("back")
        self.out_free = sem("out_free")

    def turn(self, pe):
        def fn(t, u):
            pe.wait_ge(self.src_ready, t + 3)
            pe.wait_ge(self.normed, t + 1)
            for k in range(K):
                ins = pe.transpose(self.bank[u][:, k * P:(k + 1) * P],
                                   self.src[:, u % 2, k * P:(k + 1) * P], self.ident[:, :])
            ins.then_inc(self.turned, 1)
        return fn

    def turn_back(self, pe):
        def fn(t, u):
            pe.wait_ge(self.normed, t + (1 + self.ring))
            pe.wait_ge(self.out_free, t + 1)
            for k in range(K):
                ins = pe.transpose(self.ps[2 + u % 2][:, k * P:(k + 1) * P], self.xt[:, u % 2, k, :],
                                   self.ident[:, :])
            ins.then_inc(self.back, 1)
        return fn

    def moments(self, dve):
        def fn(t, u):
            dve.wait_ge(self.turned, t + 3)
            for k in range(K):
                ins = dve.bn_stats(self.stats[:, u, k, :], self.bank[u][:, k * P:(k + 1) * P])
            ins.then_inc(self.stats_done, 1)
            dve.wait_ge(self.stats_done, t + 1)
            dve.memset(self.gate[:, 0:1], 0.0)
            for k in range(K):
                ins = dve.bn_aggr(self.mv[:, u, k, :], self.stats[:, u, k, :])
            ins.then_inc(self.mv_done, 1)
        return fn

    def scales(self, dve):
        def fn(t, u):
            dve.wait_ge(self.sd_done, t + 1)
            dve.reciprocal(self.rs[:, u, :], self.sd[:, u, :]).then_inc(self.rs_done, 1)
            dve.wait_ge(self.rs_done, t + 1)
            dve.scalar_tensor_tensor(self.nmr[:, u, :], self.mv[:, u, :, 0], -1.0, self.rs[:, u, :],
                                     ALU.mult, ALU.mult).then_inc(self.nmr_done, 1)
        return fn

    def deviations(self, act):
        def fn(t, u):
            act.wait_ge(self.mv_done, t + 1)
            act.activation(self.sd[:, u, :], self.mv[:, u, :, 1], ACT.Sqrt,
                           bias=self.epst[:, 0:1]).then_inc(self.sd_done, 1)
        return fn

    def scale(self, act):
        def fn(t, u):
            act.wait_ge(self.nmr_done, t + 1)
            act.wait_ge(self.back, t + 1)
            for k in range(K):
                ins = act.activation(self.xt[:, u % 2, k, :], self.bank[u][:, k * P:(k + 1) * P],
                                     ACT.Identity, bias=self.nmr[:, u, k:k + 1],
                                     scale=self.rs[:, u, k:k + 1])
            ins.then_inc(self.normed, 1)
        return fn

    def wait_out(self, eng, t):
        eng.wait_ge(self.back, t + 3)

    def wait_src(self, eng, t):
        eng.wait_ge(self.turned, t + 1)


def prepare(nc, ps, d, res):
    with Stage() as ctx:
        def sb(n, s, dt=F32):
            return ctx.enter_context(nc.sbuf_tensor(f"p_{n}", s, dt))

        def sem(n):
            return ctx.semaphore(nc, f"p_{n}")

        anat = sb("anat", [P, K, N])
        at = sb("at", [P, K, N])
        raw = sb("raw", [P, H1 + C1 * P])
        scr = sb("scr", [P, K, P])
        unused = sb("unused", [P, 2, K, N])
        diag4 = sb("diag4", [P, K, P])
        ones = sb("ones", [P, P])
        ahat = sb("ahat", [P, K, N])
        rsum = sb("rsum", [P, K])
        csum = sb("csum", [P, K])
        dia = sb("dia", [P, K])
        deg1 = sb("deg1", [P, K])
        deg = sb("deg", [P, K])
        sdeg = sb("sdeg", [P, K])
        dinv = sb("dinv", [P, K])
        st = sb("st", [P, B * K, 6])
        mv = sb("mv", [P, B * K, 2])
        sd = sb("sd", [P, B * K])
        ident, epst = res.ident, res.epst
        cst, idn, ain, win, vin = (sem(n) for n in ("cst", "idn", "ain", "win", "vin"))
        xin = [sem(f"xin{c}") for c in range(4)]
        plus = sem("plus")
        rcs = sem("row_column_sums")
        sums = sem("sums")
        degs = sem("degs")
        sdegs = sem("sdegs")
        dinvs = sem("dinvs")
        diags = sem("diags")
        dbc = sem("dbc")
        ah = sem("ah")
        hi = sem("hi")
        lo = sem("lo")
        stt = sem("stt")
        mvs = sem("mvs")
        sds = sem("sds")
        rss = sem("rss")
        block = ctx.block(nc)

        @block.sync
        def _(sp):
            for c in range(4):
                g = slice(c * B, (c + 1) * B)
                sp.dma_start(res.xt[:, g, :], d["x_tm"][:, g, :]).then_inc(xin[c], 16)
            sp.dma_start(anat[:], d["adj"]).then_inc(ain, 16)
            sp.dma_start(at[:], d["adjT"]).then_inc(ain, 16)
            sp.dma_start(raw[:], d["gw"]).then_inc(win, 16)
            sp.dma_start(res.vec[:], d["vec"]).then_inc(vin, 16)
            sp.wait_ge(vin, 16)

        @block.gpsimd
        def _(pool):
            pool.memset(ident[:, :], 0.0).then_inc(idn, 1)
            pool.wait_ge(idn, 1)
            pool.affine_select(out=ident[:, :], in_=ident[:, :], compare_op=ALU.not_equal, fill=1.0,
                               base=0, pattern=[[-1, P]], channel_multiplier=1).then_inc(idn, 1)
            pool.memset(epst[:, :], EPS).then_inc(cst, 1)
            pool.memset(ones[:, :], 1.0).then_inc(cst, 1)
            pool.wait_ge(ain, 32)
            pool.wait_ge(idn, 2)
            for k in range(K):
                for m in (anat, at):
                    blk = m[:, k, k * P:(k + 1) * P]
                    pool.tensor_tensor(blk, blk, ident[:, :], ALU.add).then_inc(plus, 1)

        @block.vector
        def _(dve):
            for c in range(4):
                dve.wait_ge(xin[c], 16)
                for k in range(c * B, (c + 1) * B):
                    dve.bn_stats(st[:, k, :], res.xt[:, k, :]).then_inc(stt, 1)
            dve.wait_ge(stt, B * K)
            for k in range(B * K):
                dve.bn_aggr(mv[:, k, :], st[:, k, :]).then_inc(mvs, 1)
            dve.wait_ge(plus, 2 * K)
            for k in range(K):
                dve.tensor_tensor(scr[:, k, :], anat[:, k, k * P:(k + 1) * P], ident[:, :],
                                  ALU.mult).then_inc(sums, 1)
            dve.wait_ge(sums, K)
            dve.tensor_reduce(dia[:, :], scr[:], AX.X, ALU.add).then_inc(sums, 1)
            dve.wait_ge(rcs, 2 * K)
            dve.tensor_tensor(deg1[:, :], rsum[:, :], csum[:, :], ALU.add).then_inc(sums, 1)
            dve.wait_ge(sums, 2 + K)
            dve.tensor_tensor(deg[:, :], deg1[:, :], dia[:, :], ALU.subtract).then_inc(degs, 1)
            dve.wait_ge(sdegs, 1)
            dve.reciprocal(dinv[:, :], sdeg[:, :]).then_inc(dinvs, 1)
            dve.wait_ge(dinvs, 1)
            for k in range(K):
                dve.tensor_scalar(diag4[:, k, :], ident[:, :], dinv[:, k:k + 1], None,
                                  ALU.mult).then_inc(diags, 1)
            dve.wait_ge(dbc, 1)
            for k in range(K):
                dve.scalar_tensor_tensor(ahat[:, k, :], at[:, k, :], dinv[:, k:k + 1], ps[0][:, :],
                                         ALU.mult, ALU.mult).then_inc(ah, 1)
            for k in range(K):
                dve.wait_ge(hi, k + 1)
                dve.tensor_tensor(res.ahL[:, k, :], ahat[:, k, :], res.ahH[:, k, :].bitcast(F32),
                                  ALU.subtract).then_inc(lo, 1)
            dve.wait_ge(hi, K + 1)
            dve.tensor_tensor(res.gwL[:], raw[:], res.gwH[:].bitcast(F32), ALU.subtract).then_inc(lo, 1)
            dve.wait_ge(sds, 1)
            dve.reciprocal(res.rs0[:, :], sd[:, :]).then_inc(rss, 1)
            dve.wait_ge(rss, 1)
            dve.wait_ge(mvs, B * K)
            dve.scalar_tensor_tensor(res.nmr0[:, :], mv[:, :, 0], -1.0, res.rs0[:, :],
                                     ALU.mult, ALU.mult).then_inc(rss, 1)

        @block.scalar
        def _(act):
            for k in range(K):
                for i, (m, total) in enumerate(((anat, rsum), (at, csum))):
                    act.wait_ge(plus, 2 * k + i + 1)
                    act.activation(unused[:, i, k, :], m[:, k, :], ACT.Copy,
                                   accum_out=total[:, k:k + 1]).then_inc(rcs, 1)
            act.wait_ge(degs, 1)
            act.activation(sdeg[:, :], deg[:, :], ACT.Sqrt).then_inc(sdegs, 1)
            for k in range(K):
                act.wait_ge(ah, k + 1)
                act.activation(res.ahH[:, k, :], ahat[:, k, :], ACT.Copy).then_inc(hi, 1)
            act.wait_ge(win, 16)
            act.activation(res.gwH[:], raw[:], ACT.Copy).then_inc(hi, 1)
            act.wait_ge(cst, 2)
            act.wait_ge(mvs, B * K)
            act.activation(sd[:, :], mv[:, :, 1], ACT.Sqrt, bias=epst[:, 0:1]).then_inc(sds, 1)

        @block.tensor
        def _(pe):
            pe.wait_ge(cst, 2)
            pe.wait_ge(diags, K)
            for k in range(K):
                ins = pe.matmul(ps[0][:, k * P:(k + 1) * P], ones[:, :], diag4[:, k, :],
                                start=True, stop=True)
            ins.then_inc(dbc, 1)


def three(pe, out, hi, lo, rhi, rlo, start, stop):
    pe.matmul(out, lo, rhi, start=start, stop=False)
    pe.matmul(out, hi, rlo, start=False, stop=False)
    return pe.matmul(out, hi, rhi, start=False, stop=stop)


def first_graph(nc, ps, res, Y1, d):
    with Stage() as ctx:
        def sb(n, s, dt=F32):
            return ctx.enter_context(nc.sbuf_tensor(f"b_{n}", s, dt))

        def sem(n):
            return ctx.semaphore(nc, f"b_{n}")

        xn = sb("xn", [P, 2, K, P])
        xH = sb("xH", [P, 2, K, P], F32R)
        xL = sb("xL", [P, 2, K, P], F32R)
        gH = sb("gH", [P, 2, N], F32R)
        gL = sb("gL", [P, 2, N], F32R)
        normed, xh, xl = sem("normed"), sem("xh"), sem("xl")
        agg, gh, gl, y, yev, sts = (sem(n) for n in ("agg", "gh", "gl", "y", "yev", "sts"))
        xin = sem("xin")
        block = ctx.block(nc)

        @block.sync
        def _(sp):
            sp.dma_start(res.X[:], d["x_fm"]).then_inc(xin, 16)
            sp.wait_ge(xin, 16)

        @block.scalar
        def _(act):
            act.sem_inc(gh, 2)
            act.sem_inc(yev, 2)

            def norm(t, u):
                act.wait_ge(xl, t + 1)
                for k in range(K):
                    ins = act.activation(xn[:, u, k, :], res.xt[:, bass.ds(t * K + k, 1), :],
                                         ACT.Identity, bias=res.nmr0[:, bass.ds(t * K + k, 1)],
                                         scale=res.rs0[:, bass.ds(t * K + k, 1)])
                ins.then_inc(normed, 1)
                act.wait_ge(normed, t + 1)
                act.wait_ge(agg, t + 1)
                act.activation(xH[:, u], xn[:, u], ACT.Copy).then_inc(xh, 1)

            def agg_hi(t, u):
                act.wait_ge(agg, t + 3)
                act.wait_ge(y, t + 1)
                act.activation(gH[:, u, :], ps[u][:, :], ACT.Copy).then_inc(gh, 1)

            def evac(t, u):
                act.wait_ge(y, t + 3)
                for c in range(C1):
                    ins = act.activation(Y1[:, c, cols(t)], ps[2 + 2 * u + c][:, :], ACT.Identity,
                                         bias=res.col("gb1", c))
                ins.then_inc(yev, 1)

            staggered(act, B, [(norm, 0), (agg_hi, 1), (evac, 2)])

        @block.vector
        def _(dve):
            dve.sem_inc(xl, 2)
            dve.sem_inc(gl, 2)

            def x_lo(t, u):
                dve.wait_ge(xh, t + 1)
                dve.wait_ge(agg, t + 1)
                dve.tensor_tensor(xL[:, u], xn[:, u], xH[:, u].bitcast(F32), ALU.subtract).then_inc(xl, 1)

            def agg_lo(t, u):
                dve.wait_ge(gh, t + 3)
                dve.wait_ge(y, t + 1)
                dve.tensor_tensor(gL[:, u, :], ps[u][:, :], gH[:, u, :].bitcast(F32),
                                  ALU.subtract).then_inc(gl, 1)

            def stats(t, u):
                dve.wait_ge(yev, t + 3)
                for c in range(C1):
                    ins = dve.bn_stats(res.st1[:, c, bass.ds(t, 1), :], Y1[:, c, cols(t)])
                ins.then_inc(sts, 1)

            staggered(dve, B, [(x_lo, 0), (agg_lo, 1), (stats, 2)])

        @block.tensor
        def _(pe):
            pe.sem_inc(agg, 2)
            pe.sem_inc(y, 2)

            def aggregate(t, u):
                pe.wait_ge(xl, t + 3)
                pe.wait_ge(gl, t + 1)
                for k in range(K):
                    ins = three(pe, ps[u][:, :], xH[:, u, k, :], xL[:, u, k, :], res.ahH[:, k, :],
                                res.ahL[:, k, :], k == 0, k == K - 1)
                ins.then_inc(agg, 1)

            def project(t, u):
                pe.wait_ge(gl, t + 3)
                pe.wait_ge(yev, t + 1)
                for c in range(C1):
                    ins = three(pe, ps[2 + 2 * u + c][:, :], res.gwH[:, c * P:(c + 1) * P],
                                res.gwL[:, c * P:(c + 1) * P], gH[:, u, :], gL[:, u, :], True, True)
                ins.then_inc(y, 1)

            staggered(pe, B, [(aggregate, 0), (project, 1)])


def batch_norm_scales(dve, act, sems, stats, c_n, mv, sd, rs, s, t, gamma, beta, epst, role):
    aggd, sdd, rsd, sdone, tmp, ready = sems
    if role == "dve":
        for c in range(c_n):
            dve.bn_aggr(mv[:, c, :], stats[:, c]).then_inc(aggd, 1)
        dve.wait_ge(sdd, 1)
        dve.reciprocal(rs[:, :], sd[:, :]).then_inc(rsd, 1)
        dve.wait_ge(rsd, 1)
        dve.tensor_tensor(s[:, :], rs[:, :], gamma, ALU.mult).then_inc(sdone, 1)
        dve.wait_ge(sdone, 1)
        dve.tensor_tensor(rs[:, :], mv[:, :, 0], s[:, :], ALU.mult).then_inc(tmp, 1)
        dve.wait_ge(tmp, 1)
        dve.tensor_tensor(t[:, :], beta, rs[:, :], ALU.subtract).then_inc(ready, 1)
    else:
        act.wait_ge(aggd, c_n)
        act.activation(sd[:, :], mv[:, :, 1], ACT.Sqrt, bias=epst[:, 0:1]).then_inc(sdd, 1)


def second_graph(nc, ps, res, Y1, Y2):
    with Stage() as ctx:
        def sb(n, s, dt=F32):
            return ctx.enter_context(nc.sbuf_tensor(f"c_{n}", s, dt))

        def sem(n):
            return ctx.semaphore(nc, f"c_{n}")

        mv, sd, rs = sb("mv", [P, C1, 2]), sb("sd", [P, C1]), sb("rs", [P, C1])
        s1, t1 = sb("s1", [P, C1]), sb("t1", [P, C1])
        h = sb("h", [P, 2, C1, N])
        hH = sb("hH", [P, 2, C1, N], F32R)
        hL = sb("hL", [P, 2, C1, N], F32R)
        bn = [sem(n) for n in ("bn_aggr", "bn_sd", "bn_rs", "bn_s", "bn_ms", "bn_ready")]
        hf, hh, hl, hl2, y, yev, sts = (sem(n) for n in ("hf", "hh", "hl", "hl2", "y", "yev", "sts"))
        block = ctx.block(nc)

        @block.scalar
        def _(act):
            act.sem_inc(yev, 2)
            batch_norm_scales(None, act, bn, res.st1, C1, mv, sd, rs, s1, t1, res.cols("gg1"),
                              res.cols("gbe1"), res.epst, "act")
            act.wait_ge(bn[5], 1)

            def hidden(t, u):
                act.wait_ge(hl, t + 1)
                act.wait_ge(hl2, t + 1)
                for c in range(C1):
                    ins = act.activation(h[:, u, c, :], Y1[:, c, cols(t)], ACT.Relu,
                                         bias=t1[:, c:c + 1], scale=s1[:, c:c + 1])
                ins.then_inc(hf, 1)

            def evac(t, u):
                act.wait_ge(y, t + 3)
                act.activation(Y2[:, cols(t)], ps[u][:, :], ACT.Identity,
                               bias=res.col("gb2", 0)).then_inc(yev, 1)

            staggered(act, B, [(hidden, 0), (evac, 2)])

        @block.vector
        def _(dve):
            dve.sem_inc(hl, 2)
            batch_norm_scales(dve, None, bn, res.st1, C1, mv, sd, rs, s1, t1, res.cols("gg1"),
                              res.cols("gbe1"), res.epst, "dve")

            def parts(t, u):
                dve.wait_ge(hf, t + 1)
                dve.wait_ge(y, t + 1)
                dve.tensor_copy(hH[:, u], h[:, u]).then_inc(hh, 1)
                dve.wait_ge(hh, t + 1)
                dve.tensor_tensor(hL[:, u, 0, :], h[:, u, 0, :], hH[:, u, 0, :].bitcast(F32),
                                  ALU.subtract).then_inc(hl, 1)

            def stats(t, u):
                dve.wait_ge(yev, t + 3)
                dve.bn_stats(res.st2[:, 0, bass.ds(t, 1), :], Y2[:, cols(t)]).then_inc(sts, 1)

            staggered(dve, B, [(parts, 0), (stats, 2)])

        @block.gpsimd
        def _(pool):
            pool.sem_inc(hl2, 2)

            def low(t, u):
                pool.wait_ge(hh, t + 1)
                pool.tensor_tensor(hL[:, u, 1, :], h[:, u, 1, :], hH[:, u, 1, :].bitcast(F32),
                                   ALU.subtract).then_inc(hl2, 1)

            staggered(pool, B, [(low, 0)])

        @block.tensor
        def _(pe):
            pe.sem_inc(y, 2)

            def project(t, u):
                pe.wait_ge(hl, t + 3)
                pe.wait_ge(hl2, t + 3)
                pe.wait_ge(yev, t + 1)
                for c in range(C1):
                    o = H1 + c * P
                    ins = three(pe, ps[u][:, :], res.gwH[:, o:o + P], res.gwL[:, o:o + P],
                                hH[:, u, c, :], hL[:, u, c, :], c == 0, c == C1 - 1)
                ins.then_inc(y, 1)

            staggered(pe, B, [(project, 0)])


def gate_stage(nc, ps, res, Y, fwH, fwL, d, scratch):
    with Stage() as ctx:
        def sb(n, s, dt=F32):
            return ctx.enter_context(nc.sbuf_tensor(f"d_{n}", s, dt))

        def sem(n):
            return ctx.semaphore(nc, f"d_{n}")

        ln = Norm(nc, ctx, "dln", ps, res.ident, res.epst, 4)
        mv, sd, rs = sb("mv", [P, 1, 2]), sb("sd", [P, 1]), sb("rs", [P, 1])
        s2, t2 = sb("s2", [P, 1]), sb("t2", [P, 1])
        tmp = sb("tmp", [P, 2, N])
        xg = sb("xg", [P, 2, N])
        wg = sb("wg", [P, E])
        raw = sb("raw", [P, 2, N])
        bg = sb("bg", [P, E])
        rank = sb("rank", [P, E])
        G = B * K
        sc, eq, o1, o2 = (sb(n, [P, G, E]) for n in ("sc", "eq", "o1", "o2"))
        m1, m2, mx, ex, den, p1, p2 = (sb(n, [P, G]) for n in ("m1", "m2", "mx", "ex", "den", "p1", "p2"))
        ct = sb("ct", [P, N])
        bn = [sem(n) for n in ("bn_aggr", "bn_sd", "bn_rs", "bn_s", "bn_ms", "bn_ready")]
        tmpd, xgd, xnd, gated, copied, win, gin, whi, wlo, rk = (sem(n) for n in (
            "tmpd", "xgd", "xnd", "gated", "copied", "win", "gin", "whi", "wlo", "rk"))
        step, exd, ctd, ctev, sto = (sem(n) for n in ("step", "exd", "ctd", "ctev", "sto"))
        block = ctx.block(nc)
        pieces = 2 * E * FH // N

        @block.sync
        def _(sp):
            sp.dma_start(wg[:], d["wg"]).then_inc(gin, 16)
            sp.dma_start(bg[:], d["bg"][0].partition_broadcast(P)).then_inc(gin, 16)
            for t in range(pieces):
                if t >= 2:
                    sp.wait_ge(wlo, t - 1)
                sp.dma_start(raw[:, t % 2, :], d["fw"][:, t * N:(t + 1) * N]).then_inc(win, 16)
                sp.wait_ge(win, 16 * (t + 1))
            sp.wait_ge(ctev, 1)
            sp.dma_start(scratch.rearrange("q r n -> r q n"),
                         ct[:].rearrange("r (q n) -> r q n", n=P)).then_inc(sto, 16)
            sp.wait_ge(sto, 16)

        @block.gpsimd
        def _(pool):
            for e in range(E):
                pool.memset(rank[:, e:e + 1], float(E - e)).then_inc(rk, 1)
            pool.sem_inc(copied, 2)

            def keep_x(t, u):
                pool.wait_ge(ln.src_ready, t + 3)
                pool.tensor_copy(res.X[:, cols(t)], ln.src[:, u, :]).then_inc(copied, 1)

            def weights(t, u):
                pool.wait_ge(whi, t + 1)
                pool.tensor_tensor(fwL[:, cols(t)], raw[:, u, :], fwH[:, cols(t)].bitcast(F32),
                                   ALU.subtract).then_inc(wlo, 1)

            staggered(pool, B, [(keep_x, 1), (weights, 1)])

        @block.scalar
        def _(act):
            act.sem_inc(ln.normed, ln.ring)
            act.sem_inc(ln.out_free, 2)
            batch_norm_scales(None, act, bn, res.st2, 1, mv, sd, rs, s2, t2, None, None, res.epst, "act")
            act.wait_ge(bn[5], 1)

            def normed(t, u):
                u %= 2
                act.wait_ge(ln.src_ready, t + 1)
                act.activation(tmp[:, u, :], Y[:, cols(t)], ACT.Identity, bias=t2[:, 0:1],
                               scale=s2[:, 0:1]).then_inc(tmpd, 1)

            def evac(t, u):
                u %= 2
                ln.wait_out(act, t)
                act.wait_ge(gated, t + 1)
                act.wait_ge(xnd, t + 1)
                act.activation(xg[:, u, :], ps[2 + u][:, :], ACT.Copy).then_inc(ln.out_free, 1)

            staggered(act, B, [(ln.scale(act), 3), (ln.deviations(act), 2), (normed, 0), (evac, 4)], ln.ring)
            act.wait_ge(step, 11)
            act.activation(ex[:, :], den[:, :], ACT.Exp).then_inc(exd, 1)
            act.wait_ge(ctd, 1)
            act.activation(ct[:, :], ps[5][:, :], ACT.Copy).then_inc(ctev, 1)

        @block.vector
        def _(dve):
            dve.sem_inc(ln.src_ready, 2)
            dve.sem_inc(xnd, 2)
            batch_norm_scales(dve, None, bn, res.st2, 1, mv, sd, rs, s2, t2, res.cols("gg2"),
                              res.cols("gbe2"), res.epst, "dve")

            def add(t, u):
                u %= 2
                dve.wait_ge(tmpd, t + 1)
                ln.wait_src(dve, t)
                dve.wait_ge(copied, t + 1)
                dve.tensor_tensor(ln.src[:, u, :], tmp[:, u, :], res.X[:, cols(t)],
                                  ALU.add).then_inc(ln.src_ready, 1)

            def weights_hi(t, u):
                u %= 2
                dve.wait_ge(win, t * 16 + 16)
                dve.tensor_copy(fwH[:, cols(t)], raw[:, u, :]).then_inc(whi, 1)

            def store(t, u):
                u %= 2
                dve.wait_ge(ln.out_free, t + 3)
                dve.tensor_copy(Y[:, cols(t)], xg[:, u, :]).then_inc(xnd, 1)

            staggered(dve, B, [(ln.moments(dve), 2), (add, 1), (ln.scales(dve), 2), (weights_hi, 1),
                               (store, 5)], ln.ring)

            done = [0]

            def then(ins):
                ins.then_inc(step, 1)
                done[0] += 1
                dve.wait_ge(step, done[0])

            def wide(a):
                return a.unsqueeze(2).to_broadcast([P, G, E])

            def over(a):
                return a.unsqueeze(1).to_broadcast([P, G, E])

            dve.wait_ge(gin, 32)
            dve.wait_ge(rk, E)
            dve.wait_ge(gated, B + 2)
            then(dve.tensor_tensor(sc[:], ps[4][:].rearrange("p (g e) -> p g e", e=E), over(bg[:]), ALU.add))
            then(dve.tensor_reduce(m1[:], sc[:], AX.X, ALU.max))
            then(dve.tensor_tensor(eq[:], sc[:], wide(m1[:]), ALU.is_equal))
            then(dve.tensor_tensor(eq[:], eq[:], over(rank[:]), ALU.mult))
            then(dve.tensor_reduce(mx[:], eq[:], AX.X, ALU.max))
            then(dve.tensor_tensor(o1[:], eq[:], wide(mx[:]), ALU.is_equal))
            then(dve.scalar_tensor_tensor(sc[:], o1[:], -BIG, sc[:], ALU.mult, ALU.add))
            then(dve.tensor_reduce(m2[:], sc[:], AX.X, ALU.max))
            then(dve.tensor_tensor(eq[:], sc[:], wide(m2[:]), ALU.is_equal))
            then(dve.tensor_tensor(eq[:], eq[:], over(rank[:]), ALU.mult))
            then(dve.tensor_tensor(den[:], m2[:], m1[:], ALU.subtract))
            then(dve.tensor_reduce(mx[:], eq[:], AX.X, ALU.max))
            then(dve.tensor_tensor(o2[:], eq[:], wide(mx[:]), ALU.is_equal))
            dve.wait_ge(exd, 1)
            then(dve.tensor_scalar(den[:], ex[:], 1.0, None, ALU.add))
            then(dve.reciprocal(p1[:], den[:]))
            then(dve.tensor_tensor(p2[:], ex[:], p1[:], ALU.mult))
            then(dve.tensor_tensor(o1[:], o1[:], wide(p1[:]), ALU.mult))
            then(dve.tensor_tensor(o2[:], o2[:], wide(p2[:]), ALU.mult))
            then(dve.tensor_tensor(sc[:], o1[:], o2[:], ALU.add))

        @block.tensor
        def _(pe):
            pe.sem_inc(ln.turned, 2)
            pe.sem_inc(ln.back, 2)
            pe.sem_inc(gated, 2)
            pe.wait_ge(gin, 32)

            def gate(t, u):
                u %= 2
                pe.wait_ge(ln.out_free, t + 3)
                for k in range(K):
                    ins = pe.matmul(ps[4][:, bass.ds((t * K + k) * E, E)], xg[:, u, k * P:(k + 1) * P],
                                    wg[:, :], start=True, stop=True)
                ins.then_inc(gated, 1)

            staggered(pe, B, [(ln.turn_back(pe), 4), (ln.turn(pe), 1), (gate, 5)], ln.ring)
            pe.wait_ge(step, 19)
            flat = sc[:].rearrange("p g e -> p (g e)")
            for q in range(K):
                ins = pe.transpose(ps[5][:, q * P:(q + 1) * P], flat[:, q * P:(q + 1) * P], res.ident[:, :])
            ins.then_inc(ctd, 1)


def experts(nc, ps, res, Y, fwH, fwL, scratch):
    Q = E * FJ
    R = 4
    with Stage() as ctx:
        def sb(n, s, dt=F32):
            return ctx.enter_context(nc.sbuf_tensor(f"e_{n}", s, dt))

        def sem(n):
            return ctx.semaphore(nc, f"e_{n}")

        xH, xL = sb("xH", [P, 2, N], F32R), sb("xL", [P, 2, N], F32R)
        hf = sb("hf", [P, 2, N])
        hH, hL = sb("hH", [P, R, N], F32R), sb("hL", [P, R, N], F32R)
        cb = sb("cb", [P, 2, K, E, P])
        tmp = sb("tmp", [P, 2, N])
        acc = sb("acc", [P, N])
        xh, xl = sem("x_high"), sem("x_low")
        m1, m2 = sem("hidden_sums"), sem("hidden_used")
        hfd, hha, hhd, lod = sem("hidden"), sem("high_act"), sem("high_dve"), sem("low")
        yrd, xadd, cbl, folded = sem("y_read"), sem("added"), sem("weights_in"), sem("folded")
        block = ctx.block(nc)
        cdram = scratch.rearrange("q (g e) n -> (q g) (e n)", e=E)

        @block.sync
        def _(sp):
            def load(t):
                sp.dma_start(cb[:, bass.ds(t % 2, 1)].rearrange("p o k e n -> p (o k e n)"),
                             cdram[bass.ds(t * K, K), :].rearrange("a m -> (a m)").partition_broadcast(P))\
                    .then_inc(cbl, 16)
                sp.wait_ge(cbl, t * 16 + 16)
            for t in range(B):
                if t >= 2:
                    sp.wait_ge(yrd, (t - 1) * E + 2)
                load(t)

        @block.gpsimd
        def _(pool):
            pool.sem_inc(xadd, 2)
            with pool.Fori(0, B) as t:
                for e in range(1, E):
                    pool.wait_ge(yrd, t * E + (e + 3))
                    if e == 1:
                        pool.wait_ge(folded, t + 1)
                    else:
                        pool.wait_ge(xadd, t * (E - 1) + (e + 1))
                    pool.tensor_tensor(acc[:, :], tmp[:, 0, :] if e == 1 else acc[:, :], tmp[:, e % 2, :],
                                       ALU.add).then_inc(xadd, 1)

        @block.scalar
        def _(act):
            act.sem_inc(hfd, R)
            act.sem_inc(hha, FJ - 1)
            with act.Fori(0, B) as t:
                for q in range(Q):
                    c = t * Q + q
                    e, j = q // FJ, q % FJ
                    act.wait_ge(m1, c + 1)
                    act.wait_ge(lod, c + 1)
                    ins = act.activation(hf[:, q % 2, :], ps[q % R][:, :], ACT.Relu,
                                         bias=res.col("fb1", q))
                    ins.then_inc(hfd, 1)
                    if j < FJ - 1:
                        act.wait_ge(m2, c + 1)
                        act.activation(hH[:, q % R, :], ps[q % R][:, :], ACT.Relu,
                                       bias=res.col("fb1", q)).then_inc(hha, 1)

        @block.vector
        def _(dve):
            dve.sem_inc(lod, 2)
            dve.sem_inc(yrd, 2)
            dve.sem_inc(folded, 1)

            def split_x(t):
                dve.tensor_copy(xH[:, bass.ds(t % 2, 1), :], Y[:, cols(t)].unsqueeze(1)).then_inc(xh, 1)
                dve.wait_ge(xh, t + 1)
                dve.tensor_tensor(xL[:, bass.ds(t % 2, 1), :], Y[:, cols(t)].unsqueeze(1),
                                  xH[:, bass.ds(t % 2, 1), :].bitcast(F32), ALU.subtract).then_inc(xl, 1)

            def weigh(t, e):
                dve.wait_ge(m2, t * Q + (e * FJ + FJ + R))
                dve.wait_ge(cbl, t * 16 + 16)
                dve.wait_ge(xadd, t * (E - 1) + (1, 2, 3, 3, 4, 5, 6, 7)[e])
                dve.scalar_tensor_tensor(tmp[:, e % 2, :].rearrange("p (k n) -> p k n", n=P),
                                         ps[4 + e % 2][:, :].rearrange("p (k n) -> p k n", n=P),
                                         res.col("fb2", e),
                                         cb[:, bass.ds(t % 2, 1), :, e, :].rearrange("p o k n -> p (o k) n"),
                                         ALU.add, ALU.mult).then_inc(yrd, 1)

            def fold(t):
                dve.wait_ge(xadd, t * (E - 1) + (E + 1))
                dve.tensor_tensor(res.X[:, cols(t)], res.X[:, cols(t)], acc[:, :], ALU.add)\
                    .then_inc(folded, 1)

            def body(t, first=False, last=False):
                for q in range(Q):
                    c = t * Q + q
                    e, j = q // FJ, q % FJ
                    dve.wait_ge(hfd, c + 1 + R)
                    dve.wait_ge(m2, c + 1)
                    if j == FJ - 1:
                        dve.tensor_copy(hH[:, q % R, :], hf[:, q % 2, :]).then_inc(hhd, 1)
                        dve.wait_ge(hhd, t * E + (e + 1))
                    else:
                        dve.wait_ge(hha, (t * E + e) * (FJ - 1) + (j + FJ))
                    dve.tensor_tensor(hL[:, q % R, :], hf[:, q % 2, :], hH[:, q % R, :].bitcast(F32),
                                      ALU.subtract).then_inc(lod, 1)
                    if j == FJ - 1 and (e or not first):
                        weigh(t if e else t - 1, (e - 1) % E)
                    if q == FJ + 2 and not first:
                        fold(t - 1)
                    if q == Q // 2 and not last:
                        if not first:
                            dve.wait_ge(m1, t * Q)
                        split_x(t + 1)

            split_x(0)
            body(0, first=True)
            with dve.Fori(1, B - 1) as t:
                body(t)
            body(B - 1, last=True)
            weigh(B - 1, E - 1)
            fold(B - 1)

        @block.tensor
        def _(pe):
            pe.sem_inc(m2, R)

            def first(t, q):
                c = t * Q + q
                if q == 0:
                    pe.wait_ge(xl, t + 1)
                if q % FJ < FJ - 1:
                    pe.wait_ge(hha, (t * E + q // FJ) * (FJ - 1) + (q % FJ + 1))
                else:
                    pe.wait_ge(hfd, c + 1)
                w = slice(q * P, (q + 1) * P)
                x = (xH[:, bass.ds(t % 2, 1), :], xL[:, bass.ds(t % 2, 1), :])
                three(pe, ps[q % R][:, :].unsqueeze(1), fwH[:, w], fwL[:, w], *x, True, True).then_inc(m1, 1)

            def second(t, q):
                e, j = q // FJ, q % FJ
                pe.wait_ge(lod, t * Q + (q + 3))
                if j == 0:
                    pe.wait_ge(yrd, t * E + (e + 1))
                w = slice((Q + q) * P, (Q + q + 1) * P)
                ins = three(pe, ps[4 + e % 2][:, :], fwH[:, w], fwL[:, w], hH[:, q % R, :], hL[:, q % R, :],
                            j == 0, j == FJ - 1)
                ins.then_inc(m2, 1)

            def body(t, last=False):
                for q in range(Q):
                    if q + 2 < Q:
                        first(t, q + 2)
                    elif not last:
                        first(t + 1, q + 2 - Q)
                    second(t, q)

            first(0, 0)
            first(0, 1)
            with pe.Fori(0, B - 1) as t:
                body(t)
            body(B - 1, last=True)


def third_graph(nc, ps, res, d):
    with Stage() as ctx:
        def sb(n, s, dt=F32):
            return ctx.enter_context(nc.sbuf_tensor(f"f_{n}", s, dt))

        def sem(n):
            return ctx.semaphore(nc, f"f_{n}")

        ln = Norm(nc, ctx, "fln", ps, res.ident, res.epst)
        raw = sb("raw", [P, K, N])
        aH, aL = sb("aH", [P, K, N], F32R), sb("aL", [P, K, N], F32R)
        graw = sb("graw", [P, 2, P])
        gH, gL = sb("gH", [P, 2, P], F32R), sb("gL", [P, 2, P], F32R)
        gb = sb("gb", [P, 2, P])
        xH, xL = sb("xH", [P, 2, N], F32R), sb("xL", [P, 2, N], F32R)
        zf = [sb(f"zf{y}", [P, N]) for y in range(2)]
        zH = [sb(f"zH{y}", [P, 2, N], F32R) for y in range(2)]
        zL = [sb(f"zL{y}", [P, 2, N], F32R) for y in range(2)]
        hH, hL = sb("hH", [P, 2, N], F32R), sb("hL", [P, 2, N], F32R)
        ain, gin, lin, wh, wl, lwh, lwl, bias = (sem(n) for n in (
            "adj_in", "graph_in", "lstm_in", "w_high", "w_low", "lstm_high", "lstm_low", "bias"))
        xh, hh, hl = sem("x_high"), sem("h_high"), sem("h_low")
        za = [sem(f"z_sums{y}") for y in range(2)]
        zfd = [sem(f"z{y}") for y in range(2)]
        zh = [sem(f"z_high{y}") for y in range(2)]
        zl = [sem(f"z_low{y}") for y in range(2)]
        ab = [sem(f"a_sums{y}") for y in range(2)]
        oh, ol = sem("out_high"), sem("out_low")
        block = ctx.block(nc)
        pieces = 2 * 4 * NG * P // N

        @block.sync
        def _(sp):
            sp.dma_start(raw[:], d["adjT"]).then_inc(ain, 16)
            sp.dma_start(graw[:], d["gnw"].rearrange("p (y n) -> p y n", n=P)).then_inc(gin, 16)
            for y in range(2):
                sp.dma_start(gb[:, y, :], d["gnb"][y].partition_broadcast(P)).then_inc(gin, 16)
            for t in range(pieces):
                if t < K:
                    sp.wait_ge(wl, t + 1)
                else:
                    sp.wait_ge(lwl, t - K + 1)
                sp.dma_start(raw[:, t % K, :], d["lw"][:, t * N:(t + 1) * N]).then_inc(lin, 16)
                sp.wait_ge(lin, 16 * (t + 1))

        @block.gpsimd
        def _(pool):
            pool.sem_inc(ln.src_ready, 2)

            def take(t, u):
                ln.wait_src(pool, t)
                pool.tensor_copy(ln.src[:, u, :], res.X[:, cols(t)]).then_inc(ln.src_ready, 1)

            def weights(t):
                pool.wait_ge(lin, 16 * (t + 1))
                pool.tensor_copy(res.lwH[:, t * N:(t + 1) * N], raw[:, t % K, :]).then_inc(lwh, 1)
                pool.wait_ge(lwh, t + 1)
                pool.tensor_tensor(res.lwL[:, t * N:(t + 1) * N], raw[:, t % K, :],
                                   res.lwH[:, t * N:(t + 1) * N].bitcast(F32), ALU.subtract).then_inc(lwl, 1)

            staggered(pool, B, [(take, 0)])
            for t in range(pieces):
                weights(t)

        @block.scalar
        def _(act):
            act.sem_inc(ln.normed, 2)
            act.wait_ge(ain, 16)
            for k in range(K):
                act.activation(aH[:, k, :], raw[:, k, :], ACT.Copy).then_inc(wh, 1)
            act.wait_ge(gin, 48)
            act.activation(gH[:], graw[:], ACT.Copy).then_inc(wh, 1)

            def x_hi(t, u):
                ln.wait_out(act, t)
                act.wait_ge(za[0], t + 1)
                act.activation(xH[:, u, :], ps[2 + u][:, :], ACT.Copy).then_inc(xh, 1)

            def z_hi(y):
                def fn(t, u):
                    act.wait_ge(zfd[y], t + 2)
                    act.wait_ge(ab[y], t + 1)
                    act.activation(zH[y][:, u, :], zf[y][:, :], ACT.Copy).then_inc(zh[y], 1)
                return fn

            def h_hi(t, u):
                act.wait_ge(ab[0], t + 3)
                act.wait_ge(za[1], t + 1)
                act.activation(hH[:, u, :], ps[5][:, :], ACT.Relu).then_inc(hh, 1)

            def out_hi(t, u):
                act.wait_ge(ab[1], t + 3)
                act.activation(res.HH[:, cols(t)], ps[7][:, :], ACT.Relu).then_inc(oh, 1)

            staggered(act, B, [(x_hi, 3), (ln.scale(act), 2), (h_hi, 4), (ln.deviations(act), 1),
                               (z_hi(0), 3), (out_hi, 5), (z_hi(1), 4)])

        @block.vector
        def _(dve):
            dve.sem_inc(ln.out_free, 2)
            for y in range(2):
                dve.sem_inc(zfd[y], 1)
                dve.sem_inc(zl[y], 1)
            dve.sem_inc(hl, 1)
            dve.sem_inc(ol, 1)
            for k in range(K):
                dve.wait_ge(wh, k + 1)
                dve.tensor_tensor(aL[:, k, :], raw[:, k, :], aH[:, k, :].bitcast(F32),
                                  ALU.subtract).then_inc(wl, 1)
            dve.wait_ge(wh, K + 1)
            dve.tensor_tensor(gL[:], graw[:], gH[:].bitcast(F32), ALU.subtract).then_inc(wl, 1)
            dve.tensor_tensor(res.lb[:, :], res.cols("bih"), res.cols("bhh"), ALU.add).then_inc(bias, 1)

            def x_lo(t, u):
                dve.wait_ge(xh, t + 1)
                dve.wait_ge(za[0], t + 1)
                dve.tensor_tensor(xL[:, u, :], ps[2 + u][:, :], xH[:, u, :].bitcast(F32),
                                  ALU.subtract).then_inc(ln.out_free, 1)

            def z(y):
                def fn(t, u):
                    dve.wait_ge(za[y], t + 3)
                    dve.wait_ge(zl[y], t + 1)
                    dve.tensor_tensor(zf[y][:, :].rearrange("p (k n) -> p k n", n=P),
                                      ps[4 + 2 * y][:, :].rearrange("p (k n) -> p k n", n=P),
                                      gb[:, y, :].unsqueeze(1).to_broadcast([P, K, P]),
                                      ALU.add).then_inc(zfd[y], 1)
                return fn

            def z_lo(y):
                def fn(t, u):
                    dve.wait_ge(zh[y], t + 1)
                    dve.tensor_tensor(zL[y][:, u, :], zf[y][:, :], zH[y][:, u, :].bitcast(F32),
                                      ALU.subtract).then_inc(zl[y], 1)
                return fn

            def h_lo(t, u):
                dve.wait_ge(hh, t + 1)
                dve.scalar_tensor_tensor(hL[:, u, :], ps[5][:, :], 0.0, hH[:, u, :].bitcast(F32),
                                         ALU.max, ALU.subtract).then_inc(hl, 1)

            def out_lo(t, u):
                dve.wait_ge(oh, t + 1)
                dve.scalar_tensor_tensor(res.HL[:, cols(t)], ps[7][:, :], 0.0,
                                         res.HH[:, cols(t)].bitcast(F32), ALU.max,
                                         ALU.subtract).then_inc(ol, 1)

            staggered(dve, B, [(x_lo, 3), (z_lo(1), 5), (ln.scales(dve), 2), (ln.moments(dve), 1), (h_lo, 4),
                               (z(0), 3), (z_lo(0), 3), (out_lo, 5), (z(1), 4)])

        @block.tensor
        def _(pe):
            for s in (ln.turned, ln.back, za[0], za[1], ab[0], ab[1]):
                pe.sem_inc(s, 2)

            def project(y):
                def fn(t, u):
                    pe.wait_ge(wl, K + 1)
                    if y == 0:
                        pe.wait_ge(ln.out_free, t + 3)
                    else:
                        pe.wait_ge(hl, t + 2)
                    pe.wait_ge(zfd[y], t + 1)
                    for k in range(K):
                        h, lo = ((xH, xL), (hH, hL))[y]
                        ins = three(pe, ps[4 + 2 * y][:, k * P:(k + 1) * P], h[:, u, k * P:(k + 1) * P],
                                    lo[:, u, k * P:(k + 1) * P], gH[:, y, :], gL[:, y, :], True, True)
                    ins.then_inc(za[y], 1)
                return fn

            def aggregate(y):
                def fn(t, u):
                    pe.wait_ge(zl[y], t + 2)
                    pe.wait_ge((hl, ol)[y], t + 1)
                    for k in range(K):
                        w = slice(k * P, (k + 1) * P)
                        ins = three(pe, ps[5 + 2 * y][:, :], zH[y][:, u, w], zL[y][:, u, w], aH[:, k, :],
                                    aL[:, k, :], k == 0, k == K - 1)
                    ins.then_inc(ab[y], 1)
                return fn

            staggered(pe, B, [(aggregate(0), 4), (project(0), 3), (aggregate(1), 5), (project(1), 4),
                              (ln.turn(pe), 0), (ln.turn_back(pe), 2)])


class Windows:

    def __init__(self, p, nb, groups, before, recur_before):
        self.p, self.nb, self.groups = p, nb, groups
        self.nw = S // p
        self.n = nb * self.nw
        self.chains = B // nb // groups
        self.units = [(s, c) for s in range(p) for c in range(self.chains)]
        self.before = before
        self.recur_before = recur_before
        self.after = before + groups * len(self.units)
        self.recur = groups * (p - 1) * self.chains

    def count(self, g, i):
        return g * len(self.units) + (self.before + i)

    def recurrent(self, g, i):
        return g * ((self.p - 1) * self.chains) + (self.recur_before + max(0, i - self.chains))

    def tokens(self, a, g, c, s):
        w = self.nb * S
        v = a[:, bass.ds(g * (self.chains * w) + c * w, w)]
        v = v.rearrange("q (b m) -> q b m", m=S)
        return v[:, :, s:s + self.p * (self.nw - 1) + 1:self.p]

    def shaped(self, a):
        return a.rearrange("q (b m) -> q b m", m=self.nw)


def lstms(nc, ps, res):
    R = 4
    with Stage() as ctx:
        def sb(n, s, dt=F32):
            return ctx.enter_context(nc.sbuf_tensor(f"g_{n}", s, dt))

        def sem(n):
            return ctx.semaphore(nc, f"g_{n}")

        gates = sb("gates", [P, R, NG, N])
        TC, IG, hf = sb("TC", [P, 2, N]), sb("IG", [P, 2, N]), sb("hf", [P, 2, N])
        C = sb("C", [P, 4, N])
        sH, sL = sb("sH", [P, 4, N], F32R), sb("sL", [P, 4, N], F32R)
        C1st = sb("C1", [P, 2, N])
        sums, gated, igd, fcd, cell, tcd, hfd, hhd, outd = (sem(n) for n in (
            "sums", "gated", "ig", "fc", "cell", "tanh_cell", "h", "h_high", "h_low"))
        block = ctx.block(nc)
        plan = []
        for p, nb, groups in ((1, 1, 2), (2, 2, 2), (3, 2, 2), (4, 4, 1)):
            last = plan[-1] if plan else None
            plan.append(Windows(p, nb, groups, last.after if last else 0,
                                last.recur_before + last.recur if last else 0))

        order = [(w, g, i) for w in plan for g in range(w.groups) for i in range(len(w.units))]

        def cells(w, i):
            s, c = w.units[i]
            if w.p == 1:
                return C1st[:, i % 2, 0:w.n]
            return C[:, c, 0:w.n]

        @block.tensor
        def _(pe):
            def unit(w, g, i):
                s, c = w.units[i]
                k = w.count(g, i)
                u = i % 2
                pe.wait_ge(gated, k + 1)
                if s:
                    pe.wait_ge(outd, k - w.chains + (1 + R))
                elif w.p == 2:
                    pe.wait_ge(outd, g * (2 * w.chains) + (2 * c + 2 + R))
                elif w.p == 3:
                    pe.wait_ge(outd, g * 8 + (plan[1].before + w.chains + c + 1 + R))
                elif w.p == 4:
                    o = 2 * c + 1
                    pe.wait_ge(outd, plan[2].before + 12 * (o // 4) + 8 + o % 4 + 1 + R)
                xh, xl = w.tokens(res.HH, g, c, s), w.tokens(res.HL, g, c, s)
                hh, hl = w.shaped(sH[:, c % 4, 0:w.n]), w.shaped(sL[:, c % 4, 0:w.n])
                for gate in (0, 1, 2, 3):
                    if gate == 1 and not s:
                        continue
                    bank = w.shaped(ps[4 * u + gate][:, 0:w.n])
                    o = ((w.p - 1) * NG + gate) * P
                    ins = three(pe, bank, res.lwH[:, o:o + P], res.lwL[:, o:o + P], xh, xl,
                                True, not s)
                    if s:
                        o += 4 * NG * P
                        ins = three(pe, bank, res.lwH[:, o:o + P], res.lwL[:, o:o + P], hh, hl,
                                    False, True)
                ins.then_inc(sums, 1)

            pe.sem_inc(sums, 1)
            for w, g, i in order:
                unit(w, g, i)

        @block.scalar
        def _(act):
            act.sem_inc(gated, 2)

            def tanh_cell(w, g, i):
                k, u = w.count(g, i), i % 2
                act.wait_ge(cell, k + 1)
                act.wait_ge(outd, k + (R - 1))
                act.activation(TC[:, u, 0:w.n], cells(w, i), ACT.Tanh).then_inc(tcd, 1)

            def squash(w, g, i):
                s, c = w.units[i]
                k, u = w.count(g, i), i % 2
                act.wait_ge(sums, k + 2)
                act.wait_ge(outd, k + 1)
                for gate in ((0, 2, 3) if not s else (0, 2, 1, 3)):
                    o = (w.p - 1) * NG + gate
                    ins = act.activation(gates[:, i % R, gate, 0:w.n], ps[4 * u + gate][:, 0:w.n],
                                         ACT.Tanh if gate == 2 else ACT.Sigmoid,
                                         bias=res.lb[:, o:o + 1])
                ins.then_inc(gated, 1)

            for n, (w, g, i) in enumerate(order):
                squash(w, g, i)
                if n:
                    tanh_cell(*order[n - 1])
            tanh_cell(*order[-1])

        @block.vector
        def _(dve):
            dve.sem_inc(outd, R)

            def update(w, g, i):
                s, c = w.units[i]
                k, u, n = w.count(g, i), i % 2, w.n
                dve.wait_ge(gated, k + 3)
                if not s:
                    dve.tensor_tensor(cells(w, i), gates[:, i % R, 0, 0:n], gates[:, i % R, 2, 0:n],
                                      ALU.mult).then_inc(cell, 1)
                    return
                r = w.recurrent(g, i)
                dve.tensor_tensor(IG[:, u, 0:n], gates[:, i % R, 0, 0:n], gates[:, i % R, 2, 0:n],
                                  ALU.mult).then_inc(igd, 1)
                dve.tensor_tensor(C[:, c, 0:n], gates[:, i % R, 1, 0:n], C[:, c, 0:n],
                                  ALU.mult).then_inc(fcd, 1)
                dve.wait_ge(igd, r + 1)
                dve.wait_ge(fcd, r + 1)
                dve.tensor_tensor(C[:, c, 0:n], IG[:, u, 0:n], C[:, c, 0:n], ALU.add).then_inc(cell, 1)

            def output(w, g, i):
                s, c = w.units[i]
                k, u, n = w.count(g, i), i % 2, w.n
                dve.wait_ge(tcd, k + 1)
                dve.tensor_tensor(hf[:, u, 0:n], gates[:, i % R, 3, 0:n], TC[:, u, 0:n],
                                  ALU.mult).then_inc(hfd, 1)
                if s < w.p - 1:
                    hi, lo = w.shaped(sH[:, c, 0:n]), w.shaped(sL[:, c, 0:n])
                else:
                    hi, lo = w.tokens(res.HH, g, c, s), w.tokens(res.HL, g, c, s)
                dve.wait_ge(hfd, k + 1)
                dve.tensor_copy(hi, w.shaped(hf[:, u, 0:n])).then_inc(hhd, 1)
                dve.wait_ge(hhd, k + 1)
                dve.tensor_tensor(lo, w.shaped(hf[:, u, 0:n]), hi.bitcast(F32),
                                  ALU.subtract).then_inc(outd, 1)

            for n, (w, g, i) in enumerate(order):
                update(w, g, i)
                if n:
                    output(*order[n - 1])
            output(*order[-1])


def routing(nc, ps, res, XN, d, rt):
    with Stage() as ctx:
        def sb(n, s, dt=F32):
            return ctx.enter_context(nc.sbuf_tensor(f"h_{n}", s, dt))

        def sem(n):
            return ctx.semaphore(nc, f"h_{n}")

        ln = Norm(nc, ctx, "hln", ps, res.ident, res.epst, 4)
        hs = sb("hs", [P, 2, N])
        xsum = sb("xsum", [P, B])
        wr, br = sb("wr", [P, E]), sb("br", [B, E])
        b2 = sb("b2", [E, P])
        rank, ones = sb("rank", [B, E]), sb("ones", [B, P])
        names = ("logit", "ex", "rw", "ratio", "over", "scale", "z", "ex2", "w2", "eq", "o1", "o2", "masked",
                 "dense", "idx")
        a = {n: sb(n, [B, E]) for n in names}
        col = {n: sb(n, [B, 1]) for n in ("m", "nm", "den", "rden", "m1", "m2", "x1", "x2", "e2", "p1", "p2",
                                          "i1", "i2", "dd")}
        pd = sb("pd", [B, 2, B])
        row = sb("row", [1, 2 * B])
        denseT = sb("denseT", [E, 3, B])
        hb1 = sb("hb1", [E, GH])
        hsum, copied, win, rk, xs = (sem(n) for n in ("hsum", "copied", "in", "rank", "x_sums"))
        step, acts, mm, ev = (sem(n) for n in ("step", "acts", "mm", "ev"))
        block = ctx.block(nc)

        @block.sync
        def _(sp):
            sp.dma_start(wr[:], d["wr"]).then_inc(win, 16)
            sp.dma_start(br[:], d["br"][0].partition_broadcast(B)).then_inc(win, 16)
            sp.dma_start(b2[:], d["hb2"]).then_inc(win, 16)
            sp.dma_start(hb1[:], d["hb1"]).then_inc(win, 16)
            sp.wait_ge(win, 64)

        @block.gpsimd
        def _(pool):
            for e in range(E):
                pool.memset(rank[:, e:e + 1], float(E - e)).then_inc(rk, 1)
            pool.memset(ones[:, :], 1.0).then_inc(rk, 1)
            pool.sem_inc(copied, 2)

            def keep_x(t, u):
                pool.wait_ge(ln.src_ready, t + 3)
                pool.tensor_copy(res.X[:, cols(t)], ln.src[:, u, :]).then_inc(copied, 1)

            staggered(pool, B, [(keep_x, 0)])

        @block.scalar
        def _(act):
            act.sem_inc(ln.normed, ln.ring)
            act.sem_inc(ln.out_free, 2)

            def evac(t, u):
                u %= 2
                ln.wait_out(act, t)
                act.activation(XN[:, cols(t)], ps[2 + u][:, :], ACT.Copy,
                               accum_out=xsum[:, bass.ds(t, 1)]).then_inc(ln.out_free, 1)

            staggered(act, B, [(ln.scale(act), 3), (ln.deviations(act), 2), (evac, 4)], ln.ring)
            act.wait_ge(step, 3)
            act.activation(a["ex"][:, :], a["logit"][:, :], ACT.Exp, bias=col["nm"][:, 0:1]).then_inc(acts, 1)
            act.wait_ge(step, 14)
            act.activation(a["ex2"][:, :], a["z"][:, :], ACT.Exp, bias=col["nm"][:, 0:1]).then_inc(acts, 1)
            act.wait_ge(step, 27)
            act.activation(col["e2"][:, :], col["dd"][:, :], ACT.Exp).then_inc(acts, 1)

        @block.vector
        def _(dve):
            dve.sem_inc(ln.src_ready, 2)

            def add(t, u):
                u %= 2
                dve.tensor_tensor(hs[:, u, :], res.HH[:, cols(t)].bitcast(F32),
                                  res.HL[:, cols(t)].bitcast(F32), ALU.add).then_inc(hsum, 1)
                dve.wait_ge(hsum, t + 1)
                ln.wait_src(dve, t)
                dve.wait_ge(copied, t + 1)
                dve.tensor_tensor(ln.src[:, u, :], hs[:, u, :], res.X[:, cols(t)],
                                  ALU.add).then_inc(ln.src_ready, 1)

            staggered(dve, B, [(ln.moments(dve), 2), (add, 0), (ln.scales(dve), 2)], ln.ring)

            done = [0]

            def then(ins):
                ins.then_inc(step, 1)
                done[0] += 1
                dve.wait_ge(step, done[0])

            def wide(v):
                return v[:, 0:1].to_broadcast([B, E])

            def tt(o, x, y, op):
                then(dve.tensor_tensor(o, x, y, op))

            dve.wait_ge(win, 64)
            dve.wait_ge(rk, E + 1)
            dve.wait_ge(mm, 1)
            then(dve.scalar_tensor_tensor(a["logit"][:], ps[0][0:B, 0:E], 1.0 / S, br[:, :], ALU.mult, ALU.add))
            then(dve.tensor_reduce(col["m"][:], a["logit"][:], AX.X, ALU.max))
            then(dve.tensor_scalar(col["nm"][:], col["m"][:], -1.0, None, ALU.mult))
            dve.wait_ge(acts, 1)
            then(dve.tensor_reduce(col["den"][:], a["ex"][:], AX.X, ALU.add))
            then(dve.reciprocal(col["rden"][:], col["den"][:]))
            tt(a["rw"][:], a["ex"][:], wide(col["rden"]), ALU.mult)
            dve.wait_ge(mm, 2)
            then(dve.tensor_scalar(a["scale"][:], ps[1][0:B, 0:E], float(S), None, ALU.mult))
            then(dve.reciprocal(a["ratio"][:], a["scale"][:]))
            then(dve.tensor_scalar(a["over"][:], a["scale"][:], CAP, None, ALU.is_gt))
            then(dve.tensor_scalar(a["ratio"][:], a["ratio"][:], CAP, -1.0, ALU.mult, ALU.add))
            tt(a["ratio"][:], a["ratio"][:], a["over"][:], ALU.mult)
            then(dve.scalar_tensor_tensor(a["z"][:], a["ratio"][:], 1.0, a["rw"][:], ALU.add, ALU.mult))
            then(dve.tensor_reduce(col["m"][:], a["z"][:], AX.X, ALU.max))
            then(dve.tensor_scalar(col["nm"][:], col["m"][:], -1.0, None, ALU.mult))
            dve.wait_ge(acts, 2)
            then(dve.tensor_reduce(col["den"][:], a["ex2"][:], AX.X, ALU.add))
            then(dve.reciprocal(col["rden"][:], col["den"][:]))
            tt(a["w2"][:], a["ex2"][:], wide(col["rden"]), ALU.mult)
            then(dve.tensor_reduce(col["m1"][:], a["w2"][:], AX.X, ALU.max))
            tt(a["eq"][:], a["w2"][:], wide(col["m1"]), ALU.is_equal)
            tt(a["eq"][:], a["eq"][:], rank[:, :], ALU.mult)
            then(dve.tensor_reduce(col["x1"][:], a["eq"][:], AX.X, ALU.max))
            tt(a["o1"][:], a["eq"][:], wide(col["x1"]), ALU.is_equal)
            then(dve.scalar_tensor_tensor(a["masked"][:], a["o1"][:], -BIG, a["w2"][:], ALU.mult, ALU.add))
            then(dve.tensor_reduce(col["m2"][:], a["masked"][:], AX.X, ALU.max))
            tt(a["eq"][:], a["masked"][:], wide(col["m2"]), ALU.is_equal)
            tt(a["eq"][:], a["eq"][:], rank[:, :], ALU.mult)
            tt(col["dd"][:], col["m2"][:], col["m1"][:], ALU.subtract)
            then(dve.tensor_reduce(col["x2"][:], a["eq"][:], AX.X, ALU.max))
            tt(a["o2"][:], a["eq"][:], wide(col["x2"]), ALU.is_equal)
            dve.wait_ge(acts, 3)
            then(dve.tensor_scalar(col["den"][:], col["e2"][:], 1.0, None, ALU.add))
            then(dve.reciprocal(col["p1"][:], col["den"][:]))
            tt(col["p2"][:], col["e2"][:], col["p1"][:], ALU.mult)
            tt(a["eq"][:], a["o1"][:], wide(col["p1"]), ALU.mult)
            tt(a["masked"][:], a["o2"][:], wide(col["p2"]), ALU.mult)
            tt(a["dense"][:], a["eq"][:], a["masked"][:], ALU.add)
            then(dve.tensor_scalar(col["i1"][:], col["x1"][:], -1.0, float(E), ALU.mult, ALU.add))
            then(dve.tensor_scalar(col["i2"][:], col["x2"][:], -1.0, float(E), ALU.mult, ALU.add))
            then(dve.tensor_scalar(pd[:, 0, :], res.ident[0:B, 0:B], col["p1"][:, 0:1], None, ALU.mult))
            then(dve.tensor_scalar(pd[:, 1, :], res.ident[0:B, 0:B], col["p2"][:, 0:1], None, ALU.mult))
            dve.wait_ge(mm, 3)
            then(dve.tensor_copy(rt.index[:, :], ps[2][0:1, 0:2 * B]))
            then(dve.tensor_copy(rt.weight[:].rearrange("p x b -> p (x b)"), ps[3][:, 0:2 * B]))
            then(dve.tensor_copy(denseT[:].rearrange("e x b -> e (x b)"), ps[4][0:E, 0:3 * B]))
            dve.wait_ge(mm, 4)
            then(dve.tensor_copy(rt.bias2[:, :], ps[5][:, 0:B]))
            for x in range(2):
                then(dve.tensor_copy(rt.bias1[:, x * GJ:(x + 1) * GJ].rearrange("p f b -> p (f b)"),
                                     ps[6][:, x * GJ * B:(x + 1) * GJ * B]))

        @block.tensor
        def _(pe):
            pe.sem_inc(ln.turned, 2)
            pe.sem_inc(ln.back, 2)
            staggered(pe, B, [(ln.turn(pe), 1), (ln.turn_back(pe), 4)], ln.ring)
            pe.wait_ge(win, 64)
            pe.wait_ge(ln.out_free, B + 2)
            pe.matmul(ps[0][0:B, 0:E], xsum[:, :], wr[:, :], start=True, stop=True).then_inc(mm, 1)
            pe.wait_ge(rk, E + 1)
            pe.wait_ge(step, 6)
            pe.matmul(ps[1][0:B, 0:E], ones[:, 0:B], a["rw"][:, :], start=True, stop=True).then_inc(mm, 1)
            pe.wait_ge(step, 39)
            for x, c in enumerate(("i1", "i2")):
                pe.matmul(ps[2][0:1, x * B:(x + 1) * B], col[c][:, 0:1], res.ident[0:B, 0:B],
                          start=True, stop=True)
            pe.matmul(ps[3][:, 0:2 * B], ones[:, :], pd[:].rearrange("p x b -> p (x b)"), start=True, stop=True)
            for x, n in enumerate(("o1", "o2", "dense")):
                ins = pe.transpose(ps[4][0:E, x * B:(x + 1) * B], a[n][:, :], res.ident[0:B, 0:B])
            ins.then_inc(mm, 1)
            pe.wait_ge(step, 42)
            for x in range(2):
                for f in range(GJ):
                    o = (x * GJ + f) * B
                    pe.matmul(ps[6][:, o:o + B], hb1[:, f * P:(f + 1) * P], denseT[:, x, :],
                              start=True, stop=True)
            pe.matmul(ps[5][:, 0:B], b2[:, :], denseT[:, 2, :], start=True, stop=True).then_inc(mm, 1)


def chosen_experts(nc, ps, res, XN, d, rt):
    F = 2 * GJ
    with Stage() as ctx:
        def sb(n, s, dt=F32):
            return ctx.enter_context(nc.sbuf_tensor(f"i_{n}", s, dt))

        def sem(n):
            return ctx.semaphore(nc, f"i_{n}")

        raw = [sb(f"raw{h}", [P, 2, 2, GH]) for h in (1, 2)]
        wH = [sb(f"wH{h}", [P, 2, 2, GH], F32R) for h in (1, 2)]
        wL = [sb(f"wL{h}", [P, 2, 2, GH], F32R) for h in (1, 2)]
        xH, xL = sb("xH", [P, 2, N], F32R), sb("xL", [P, 2, N], F32R)
        hf = sb("hf", [P, F, N])
        hH, hL = sb("hH", [P, F, N], F32R), sb("hL", [P, F, N], F32R)
        b1 = sb("b1", [P, 2, F])
        b1d = sem("hidden_bias")
        win = [[sem(f"weights{h}_{n}") for n in ("even", "odd")] for h in (1, 2)]
        wh, wl = [sem("w_high1"), sem("w_high2")], [sem("w_low1"), sem("w_low2")]
        scaled, xh, xl = (sem(n) for n in ("scaled", "x_high", "x_low"))
        m1, m2, hfd, hhd, lod, outd = (sem(n) for n in ("hidden_sums", "hidden_used", "hidden", "h_high",
                                                        "h_low", "out"))
        block = ctx.block(nc)

        @block.sync
        def _(sp):
            for t in range(B):
                e = [sp.value_load(rt.index[0:1, bass.ds(x * B + t, 1)], min_val=0, max_val=E - 1)
                     for x in range(2)]
                for h in range(2):
                    if t >= 2:
                        sp.wait_ge(wl[h], t - 1)
                    for x in range(2):
                        sp.dma_start(raw[h][:, t % 2, x, :],
                                     d["hw"][bass.ds(e[x], 1), :, h * GH:(h + 1) * GH]
                                     .rearrange("o p n -> (o p) n")).then_inc(win[h][t % 2], 16)

        @block.gpsimd
        def _(pool):
            def low(h):
                def fn(t, u):
                    pool.wait_ge(wh[h], t + 1)
                    pool.tensor_tensor(wL[h][:, u], raw[h][:, u], wH[h][:, u].bitcast(F32),
                                       ALU.subtract).then_inc(wl[h], 1)
                return fn

            staggered(pool, B, [(low(0), 0), (low(1), 0)])

        @block.scalar
        def _(act):
            def hidden(t, u):
                act.wait_ge(b1d, t + 1)
                for q in range(F):
                    act.wait_ge(m1, t * F + (q + 1 + 2 * F))
                    act.wait_ge(lod, t * F + (q + 1))
                    act.activation(hf[:, q, :], ps[q][:, :], ACT.Gelu, bias=b1[:, u, q:q + 1])\
                        .then_inc(hfd, 1)
                    act.wait_ge(m2, t * F + (q + 1 + F))
                    act.activation(hH[:, q, :], ps[q][:, :], ACT.Gelu, bias=b1[:, u, q:q + 1])\
                        .then_inc(hhd, 1)

            staggered(act, B, [(hidden, 1)])

        @block.vector
        def _(dve):
            dve.sem_inc(lod, F)
            dve.sem_inc(outd, 2)

            def layer_1(t, u):
                dve.wait_ge(win[0][u], t * 16 + (32 - 16 * u))
                dve.wait_ge(m1, t * F + F)
                dve.tensor_copy(wH[0][:, u], raw[0][:, u]).then_inc(wh[0], 1)

            def layer_2(t, u):
                dve.wait_ge(win[1][u], t * 16 + (32 - 16 * u))
                for x in range(2):
                    w2 = raw[1][:, u, x, :]
                    ins = dve.tensor_scalar(w2, w2, rt.weight[:, x, bass.ds(t, 1)], None, ALU.mult)
                ins.then_inc(scaled, 1)
                dve.wait_ge(scaled, t + 1)
                dve.wait_ge(m2, t * F + F)
                dve.tensor_copy(wH[1][:, u], raw[1][:, u]).then_inc(wh[1], 1)

            def x_parts(t, u):
                dve.tensor_copy(b1[:, u, :], rt.bias1[:, :, bass.ds(t, 1)].rearrange("p q o -> p (q o)"))\
                    .then_inc(b1d, 1)
                dve.wait_ge(m1, t * F + F)
                dve.tensor_copy(xH[:, u, :], XN[:, cols(t)]).then_inc(xh, 1)
                dve.wait_ge(xh, t + 1)
                dve.tensor_tensor(xL[:, u, :], XN[:, cols(t)], xH[:, u, :].bitcast(F32),
                                  ALU.subtract).then_inc(xl, 1)

            def low(q):
                def fn(t, u):
                    dve.wait_ge(hfd, t * F + (q + 1))
                    dve.wait_ge(hhd, t * F + (q + 1))
                    dve.wait_ge(m2, t * F + (q + 1 + F))
                    dve.tensor_tensor(hL[:, q, :], hf[:, q, :], hH[:, q, :].bitcast(F32),
                                      ALU.subtract).then_inc(lod, 1)
                return fn

            def add(t, u):
                dve.wait_ge(m2, t * F + 3 * F)
                dve.scalar_tensor_tensor(XN[:, cols(t)], ps[4 + u][:, :], rt.bias2[:, bass.ds(t, 1)],
                                         XN[:, cols(t)], ALU.add, ALU.add).then_inc(outd, 1)

            staggered(dve, B, [(layer_1, 0), (low(0), 1), (x_parts, 0), (low(1), 1), (layer_2, 0),
                               (low(2), 1), (add, 2), (low(3), 1)])

        @block.tensor
        def _(pe):
            pe.sem_inc(m1, 2 * F)
            pe.sem_inc(m2, 2 * F)

            def first(q):
                def fn(t, u):
                    x, f = q // GJ, q % GJ
                    if q == 0:
                        pe.wait_ge(wl[0], t + 1)
                        pe.wait_ge(xl, t + 1)
                    pe.wait_ge(lod, t * F + (q + 1))
                    w = slice(f * P, (f + 1) * P)
                    three(pe, ps[q][:, :], wH[0][:, u, x, w], wL[0][:, u, x, w], xH[:, u, :], xL[:, u, :],
                          True, True).then_inc(m1, 1)
                return fn

            def second(q):
                def fn(t, u):
                    x, f = q // GJ, q % GJ
                    pe.wait_ge(lod, t * F + (q + 1 + F))
                    if q == 0:
                        pe.wait_ge(wl[1], t + 1)
                    w = slice(f * P, (f + 1) * P)
                    three(pe, ps[4 + u][:, :], wH[1][:, u, x, w], wL[1][:, u, x, w], hH[:, q, :], hL[:, q, :],
                          q == 0, q == F - 1).then_inc(m2, 1)
                return fn

            staggered(pe, B, [(first(0), 1), (second(2), 2), (first(1), 1), (second(3), 2),
                              (first(2), 1), (second(0), 1), (first(3), 1), (second(1), 1)])


def final_norm(nc, ps, res, XN, out):
    with Stage() as ctx:
        def sb(n, s, dt=F32):
            return ctx.enter_context(nc.sbuf_tensor(f"j_{n}", s, dt))

        def sem(n):
            return ctx.semaphore(nc, f"j_{n}")

        ln = Norm(nc, ctx, "jln", ps, res.ident, res.epst, 4)
        z, o = sb("z", [P, 2, N]), sb("o", [P, ln.ring, N])
        addd, stored = sem("added"), [sem(f"stored{u}") for u in range(ln.ring)]
        block = ctx.block(nc)

        @block.sync
        def _(sp):
            for u in range(ln.ring):
                sp.sem_inc(stored[u], 16)
            for t in range(B):
                sp.wait_ge(addd, t + 3)
                sp.dma_start(out[:, t * N:(t + 1) * N], o[:, t % ln.ring, :]).then_inc(stored[t % ln.ring], 16)
            for u in range(ln.ring):
                sp.wait_ge(stored[u], 16 * (B // ln.ring + 1))

        @block.gpsimd
        def _(pool):
            pool.sem_inc(ln.src_ready, 2)

            def take(t, u):
                ln.wait_src(pool, t)
                pool.tensor_copy(ln.src[:, u, :], XN[:, cols(t)]).then_inc(ln.src_ready, 1)

            staggered(pool, B, [(take, 0)])

        @block.scalar
        def _(act):
            act.sem_inc(ln.normed, ln.ring)
            act.sem_inc(ln.out_free, 2)

            def affine(t, u):
                u %= 2
                ln.wait_out(act, t)
                act.wait_ge(addd, t + 1)
                act.activation(z[:, u, :], ps[2 + u][:, :], ACT.Identity, bias=res.col("beta", 0),
                               scale=res.col("gamma", 0)).then_inc(ln.out_free, 1)

            staggered(act, B, [(ln.scale(act), 2), (ln.deviations(act), 1), (affine, 4)], ln.ring)

        @block.vector
        def _(dve):
            dve.sem_inc(addd, 2)

            def add(t, u):
                dve.wait_ge(ln.out_free, t + 3)
                dve.wait_ge(stored[u], t * (16 // ln.ring) + (16 - 16 // ln.ring * u))
                dve.tensor_tensor(o[:, u, :], z[:, u % 2, :], res.X[:, cols(t)], ALU.add).then_inc(addd, 1)

            staggered(dve, B, [(ln.moments(dve), 1), (ln.scales(dve), 1), (add, 5)], ln.ring)

        @block.tensor
        def _(pe):
            pe.sem_inc(ln.turned, 2)
            pe.sem_inc(ln.back, 2)
            staggered(pe, B, [(ln.turn(pe), 0), (ln.turn_back(pe), 3)], ln.ring)


class Resident:

    def col(self, name, i):
        a = VEC[name][0] + i
        return self.vec[:, a:a + 1]

    def cols(self, name):
        a, b = VEC[name]
        return self.vec[:, a:b]


def build(nc, d, out):
    with ExitStack() as ctx:
        def keep(c, name, shape, dt=F32):
            return c.enter_context(nc.sbuf_tensor(name, shape, dt))

        ps = [ctx.enter_context(nc.psum_tensor(f"bank{i}", [P, N], F32)) for i in range(8)]
        res = Resident()
        res.X = keep(ctx, "X", [P, TOK])
        res.vec = keep(ctx, "vec", [P, NVEC])
        res.ident = keep(ctx, "ident", [P, P])
        res.epst = keep(ctx, "epst", [P, 1])
        with ExitStack() as first:
            Y2 = keep(first, "Y2", [P, TOK])
            res.xt = Y2[:].rearrange("p (t n) -> p t n", n=P)
            res.st2 = keep(first, "st2", [P, 1, B, 6])
            with ExitStack() as graph:
                res.gwH = keep(graph, "gwH", [P, H1 + C1 * P], F32R)
                res.gwL = keep(graph, "gwL", [P, H1 + C1 * P], F32R)
                res.st1 = keep(graph, "st1", [P, C1, B, 6])
                res.ahH = keep(graph, "ahH", [P, K, N], F32R)
                res.ahL = keep(graph, "ahL", [P, K, N], F32R)
                res.rs0 = keep(graph, "rs0", [P, B * K])
                res.nmr0 = keep(graph, "nmr0", [P, B * K])
                prepare(nc, ps, d, res)
                Y1 = keep(graph, "Y1", [P, C1, TOK])
                first_graph(nc, ps, res, Y1, d)
                second_graph(nc, ps, res, Y1, Y2)
            fwH = keep(first, "fwH", [P, 2 * E * FH], F32R)
            fwL = keep(first, "fwL", [P, 2 * E * FH], F32R)
            combine = nc.dram_tensor("combine", [K, P, P], F32, kind="Internal").ap()
            gate_stage(nc, ps, res, Y2, fwH, fwL, d, combine)
            experts(nc, ps, res, Y2, fwH, fwL, combine)
        res.HH = keep(ctx, "HH", [P, TOK], F32R)
        res.HL = keep(ctx, "HL", [P, TOK], F32R)
        with ExitStack() as recurrent:
            res.lwH = keep(recurrent, "lwH", [P, 2 * 4 * NG * P], F32R)
            res.lwL = keep(recurrent, "lwL", [P, 2 * 4 * NG * P], F32R)
            res.lb = keep(recurrent, "lb", [P, 4 * NG])
            third_graph(nc, ps, res, d)
            lstms(nc, ps, res)
        XN = keep(ctx, "XN", [P, TOK])
        rt = Resident()
        rt.index = keep(ctx, "index", [1, 2 * B], I32)
        rt.weight = keep(ctx, "weight", [P, 2, B])
        rt.bias1 = keep(ctx, "bias1", [P, 2 * GJ, B])
        rt.bias2 = keep(ctx, "bias2", [P, B])
        routing(nc, ps, res, XN, d, rt)
        chosen_experts(nc, ps, res, XN, d, rt)
        final_norm(nc, ps, res, XN, out)


def _layouts(i):
    import numpy as np
    c = np.ascontiguousarray
    x = i["x"]
    a = {
        "x_tm": c(x.reshape(B * K, P, D).transpose(1, 0, 2)),
        "x_fm": c(x.reshape(TOK, D).T),
        "adj": c(i["adj"].reshape(K, P, S).transpose(1, 0, 2)),
        "adjT": c(i["adj"].T.reshape(K, P, S).transpose(1, 0, 2)),
        "gw": c(np.concatenate([i["L0_gnn_W1"].T,
                                i["L0_gnn_W2"].T.reshape(C1, P, P).transpose(1, 0, 2).reshape(P, C1 * P)], 1)),
        "fw": c(np.concatenate([i["L0_ffn_W1"].transpose(2, 0, 1).reshape(P, E * FH),
                                i["L0_ffn_W2"].transpose(2, 0, 1).reshape(FJ, P, E, P).transpose(1, 2, 0, 3)
                                .reshape(P, E * FH)], 1)),
        "wg": c(i["L0_ffn_Wg"].T),
        "bg": c(i["L0_ffn_bg"].reshape(1, E)),
        "gnw": c(np.concatenate([i["L1_gnn_Wg0"], i["L1_gnn_Wg1"]], 1)),
        "gnb": c(np.stack([i["L1_gnn_bg0"], i["L1_gnn_bg1"]])),
        "lw": c(np.concatenate([i["L1_gnn_Wih"].transpose(2, 0, 1).reshape(P, 4 * NG * P),
                                i["L1_gnn_Whh"].transpose(2, 0, 1).reshape(P, 4 * NG * P)], 1)),
        "wr": c(i["L1_ffn_Wr"]),
        "br": c(i["L1_ffn_br"].reshape(1, E)),
        "hw": c(np.concatenate([i["L1_ffn_W1"].reshape(E, P, GH),
                                i["L1_ffn_W2"].reshape(E, GJ, P, P).transpose(0, 2, 1, 3).reshape(E, P, GH)], 2)),
        "hb1": c(i["L1_ffn_b1"]),
        "hb2": c(i["L1_ffn_b2"]),
    }
    vec = {
        "gb1": i["L0_gnn_b1"].reshape(C1, P).T, "gg1": i["L0_gnn_g1"].reshape(C1, P).T,
        "gbe1": i["L0_gnn_be1"].reshape(C1, P).T, "gb2": i["L0_gnn_b2"][:, None],
        "gg2": i["L0_gnn_g2"][:, None], "gbe2": i["L0_gnn_be2"][:, None],
        "fb1": i["L0_ffn_b1"].reshape(E * FJ, P).T, "fb2": i["L0_ffn_b2"].T,
        "bih": i["L1_gnn_bih"].reshape(4 * NG, P).T, "bhh": i["L1_gnn_bhh"].reshape(4 * NG, P).T,
        "gamma": i["L1_ffn_gamma"][:, None], "beta": i["L1_ffn_beta"][:, None],
    }
    a["vec"] = c(np.concatenate([vec[n] for n in VEC], 1))
    return a


def kernel(**inputs):
    import numpy as _np
    import concourse.bacc as _bacc
    from concourse import mybir as _mybir
    from concourse.bass_utils import run_bass_kernel_spmd as _run

    nc = _bacc.Bacc("TRN2", target_bir_lowering=False, num_devices=1)
    arrays, args = {}, {}
    for name, a in _layouts({k: _np.asarray(v) for k, v in inputs.items()}).items():
        arrays[f"in_{name}"] = a
        args[name] = nc.dram_tensor(f"in_{name}", a.shape, _mybir.dt.from_np(a.dtype), kind="ExternalInput").ap()
    out = nc.dram_tensor("out_x", (P, TOK), _mybir.dt.float32, kind="ExternalOutput").ap()
    build(nc, args, out)
    r = _run(nc, [arrays], core_ids=[0])
    return _np.ascontiguousarray(r.results[0]["out_x"].T).reshape(B, S, D)
```
